# Optimizing a Trainium2 kernel written in Bass

```python
import numpy as np
import jax
import jax.numpy as jnp

def _softmax(x, axis=-1):
    return jax.nn.softmax(x, axis=axis)

def _gelu(x):
    return jax.nn.gelu(x, approximate=True)

def _silu(x):
    return jax.nn.silu(x)

def _sigmoid(x):
    return jax.nn.sigmoid(x)

def _layernorm(x, axis=-1, eps=1e-05):
    m = jnp.mean(x, axis=axis, keepdims=True)
    v = jnp.var(x, axis=axis, keepdims=True)
    return (x - m) / jnp.sqrt(v + eps)

def _scatter_add(tgt, idx, src, axis=0):
    return tgt.at[idx].add(src)

def _segment_sum(src, seg, n):
    return jax.ops.segment_sum(src, seg, n)
kernel_name = 'mk_adj_resnorm_d4_adj_r2_9ef2d0'

def setup_inputs(seed: int=0):
    np.random.seed(seed)
    _w = jnp.asarray

    def _rec_inputs():
        import jax
        import jax.numpy as jnp
        _gk = jax.random.key(seed)
        x = 0.0001732 + 1 * jax.random.normal(jax.random.fold_in(_gk, 1), (5120, 64), jnp.float32)
        _a = jax.random.bernoulli(jax.random.fold_in(_gk, 2), 0.003125, (5120, 5120))
        _af = _a.astype(jnp.float32)
        _af = _af * jax.random.uniform(jax.random.fold_in(_gk, 3), (5120, 5120), jnp.float32, 0.05, 0.02)
        adj = _af
        return (x, adj)
    x, adj = _rec_inputs()

    def _L0_gnn_setup():
        import jax, jax.numpy as jnp
        import numpy as np
        N_USERS = 2048
        N_ITEMS = 3072
        EMB = 64
        LN_EPS = 1e-05
        key = jax.random.key(seed)
        ks = jax.random.split(key, 10)
        N = N_USERS + N_ITEMS
        ego = jax.random.normal(ks[0], (N, EMB), jnp.float32)
        adj = (jax.random.uniform(ks[1], (N, N), jnp.float32) < 0.01).astype(jnp.float32) * 0.02
        xav = float(np.sqrt(6.0 / (EMB + EMB)))
        W_u = jax.random.uniform(ks[2], (EMB, EMB), jnp.float32, -xav, xav)
        W_i = jax.random.uniform(ks[3], (EMB, EMB), jnp.float32, -xav, xav)
        diag_u = jax.random.uniform(ks[4], (N_USERS,), jnp.float32, 0.99, 1.01)
        diag_i = jax.random.uniform(ks[5], (N_ITEMS,), jnp.float32, 0.99, 1.01)
        par_u = jax.random.uniform(ks[6], (2,), jnp.float32, 0.0, 0.99)
        par_i = jax.random.uniform(ks[7], (2,), jnp.float32, 0.0, 0.99)
        ln_gamma = jnp.ones((EMB,), jnp.float32)
        ln_beta = jnp.zeros((EMB,), jnp.float32)
        return {'ego_embeddings': ego, 'adj': adj, 'W_u': W_u, 'diag_u': diag_u, 'par_u': par_u, 'W_i': W_i, 'diag_i': diag_i, 'par_i': par_i, 'ln_gamma': ln_gamma, 'ln_beta': ln_beta}
    _L0_gnn_all = _L0_gnn_setup()
    _L0_gnn_in = {k: v for k, v in _L0_gnn_all.items() if k in ('W_u', 'diag_u', 'par_u', 'W_i', 'diag_i', 'par_i', 'ln_gamma', 'ln_beta')}
    del _L0_gnn_all

    def _L1_gnn_setup():
        import jax, jax.numpy as jnp
        import numpy as np
        N = 8192
        F_IN = 64
        F_OUT = 64
        key = jax.random.key(seed)
        k1, k2, k3 = jax.random.split(key, 3)
        x = jax.random.normal(k1, (N, F_IN), dtype=jnp.float32)
        adj = jax.random.randint(k2, (N, N), 0, 2).astype(jnp.float32)
        W = jax.random.normal(k3, (F_IN, F_OUT), dtype=jnp.float32) * (1.0 / np.sqrt(F_IN))
        b = jnp.zeros((F_OUT,), dtype=jnp.float32)
        return {'x': x, 'adj': adj, 'W': W, 'b': b}
    _L1_gnn_all = _L1_gnn_setup()
    _L1_gnn_in = {k: v for k, v in _L1_gnn_all.items() if k in ('W', 'b')}
    del _L1_gnn_all

    def _L2_gnn_setup():
        import jax, jax.numpy as jnp
        import numpy as np
        N = 5000
        DIM = 64
        F_CONST = 1.0
        B_CONST = 0.1
        R_CONST = 0.01
        key = jax.random.key(seed)
        k1, k2 = jax.random.split(key)
        t = jnp.zeros((1,), dtype=jnp.float32)
        x = jax.random.uniform(k1, (N, DIM), dtype=jnp.float32)
        A = jax.random.uniform(k2, (N, N), dtype=jnp.float32)
        return {'t': t, 'x': x, 'A': A}
    _L2_gnn_all = _L2_gnn_setup()
    _L2_gnn_in = {k: v for k, v in _L2_gnn_all.items() if k in ('t',)}
    del _L2_gnn_all

    def _L3_gnn_setup():
        import jax, jax.numpy as jnp
        import numpy as np
        N, D_IN, D_OUT = (4096, 64, 64)
        MAX_NEIGH = 100
        DECAY = 0.5
        key = jax.random.key(seed)
        k1, k2, k3, k4 = jax.random.split(key, 4)
        stdv = 1.0 / np.sqrt(D_OUT)
        inputs = {'input': jax.random.normal(k1, (N, D_IN), dtype=jnp.float32), 'adj': jax.random.randint(k2, (N, N), 0, 2).astype(jnp.float32), 'weight': jax.random.uniform(k3, (D_IN, D_OUT), minval=-stdv, maxval=stdv, dtype=jnp.float32), 'bias': jax.random.uniform(k4, (D_OUT,), minval=-stdv, maxval=stdv, dtype=jnp.float32)}
        return inputs
    _L3_gnn_all = _L3_gnn_setup()
    _L3_gnn_in = {k: v for k, v in _L3_gnn_all.items() if k in ('weight', 'bias')}
    del _L3_gnn_all
    return {'x': x, 'adj': adj, 'L0_gnn_W_u': _L0_gnn_in['W_u'], 'L0_gnn_diag_u': _L0_gnn_in['diag_u'], 'L0_gnn_par_u': _L0_gnn_in['par_u'], 'L0_gnn_W_i': _L0_gnn_in['W_i'], 'L0_gnn_diag_i': _L0_gnn_in['diag_i'], 'L0_gnn_par_i': _L0_gnn_in['par_i'], 'L0_gnn_ln_gamma': _L0_gnn_in['ln_gamma'], 'L0_gnn_ln_beta': _L0_gnn_in['ln_beta'], 'L1_gnn_W': _L1_gnn_in['W'], 'L1_gnn_b': _L1_gnn_in['b'], 'L2_gnn_t': _L2_gnn_in['t'], 'L3_gnn_weight': _L3_gnn_in['weight'], 'L3_gnn_bias': _L3_gnn_in['bias']}

def reference(x, adj, L0_gnn_W_u, L0_gnn_diag_u, L0_gnn_par_u, L0_gnn_W_i, L0_gnn_diag_i, L0_gnn_par_i, L0_gnn_ln_gamma, L0_gnn_ln_beta, L1_gnn_W, L1_gnn_b, L2_gnn_t, L3_gnn_weight, L3_gnn_bias):
    import jax
    import jax.numpy as jnp

    def _L0_gnn_ref(ego_embeddings, adj, W_u, diag_u, par_u, W_i, diag_i, par_i, ln_gamma, ln_beta):
        import jax, jax.numpy as jnp
        import numpy as np
        N_USERS = 2048
        N_ITEMS = 3072
        EMB = 64
        LN_EPS = 1e-05
        nu = diag_u.shape[0]
        res = ego_embeddings
        ego_u = ego_embeddings[:nu]
        ego_i = ego_embeddings[nu:]
        u = par_u[0] * par_u[1] * (diag_u[:, None] * ego_u @ W_u) + ego_u
        i = par_i[0] * par_i[1] * (diag_i[:, None] * ego_i @ W_i) + ego_i
        e = jnp.concatenate([u, i], axis=0)
        h = adj @ (adj.T @ e)
        mu = jnp.mean(h, axis=-1, keepdims=True)
        var = jnp.var(h, axis=-1, keepdims=True)
        out = (h - mu) * jax.lax.rsqrt(var + LN_EPS) * ln_gamma + ln_beta + res
        return out

    def _L1_gnn_ref(x, adj, W, b):
        import jax, jax.numpy as jnp
        import numpy as np
        N = 8192
        F_IN = 64
        F_OUT = 64
        deg = adj.sum(axis=0) + 1.0
        dinv = jnp.where(deg > 0, jax.lax.rsqrt(deg), 0.0)
        xw = x @ W
        z = dinv[:, None] * xw
        out = dinv[:, None] * (adj.T @ z + z) + b
        return jax.nn.relu(out)

    def _L2_gnn_ref(t, x, A):
        import jax, jax.numpy as jnp
        import numpy as np
        N = 5000
        DIM = 64
        F_CONST = 1.0
        B_CONST = 0.1
        R_CONST = 0.01
        Ax = A @ x
        outer = R_CONST * jnp.sum(x * Ax, axis=1, keepdims=True)
        return F_CONST - B_CONST * x - outer

    def _L3_gnn_ref(input, adj, weight, bias):
        import jax, jax.numpy as jnp
        import numpy as np
        N, D_IN, D_OUT = (4096, 64, 64)
        MAX_NEIGH = 100
        DECAY = 0.5
        support = input @ weight
        mask = (adj != 0).astype(support.dtype)
        rank = jnp.cumsum(mask, axis=1)
        deg = rank[:, -1:]
        k = jnp.minimum(deg, float(MAX_NEIGH))
        pos = rank - (deg - k)
        w = mask * jnp.where(pos > 0, DECAY ** (k - pos), 0.0)
        out = w @ support + bias
        return out
    x = _layernorm(x + _L0_gnn_ref(x, adj, L0_gnn_W_u, L0_gnn_diag_u, L0_gnn_par_u, L0_gnn_W_i, L0_gnn_diag_i, L0_gnn_par_i, L0_gnn_ln_gamma, L0_gnn_ln_beta), axis=-1)
    x = _layernorm(x + _L1_gnn_ref(x, adj, L1_gnn_W, L1_gnn_b), axis=-1)
    x = _layernorm(x + _L2_gnn_ref(L2_gnn_t, x, adj), axis=-1)
    x = _layernorm(x + _L3_gnn_ref(x, adj, L3_gnn_weight, L3_gnn_bias), axis=-1)
    return x

_drawn_inputs = setup_inputs


def setup_inputs(seed=0):
    import zlib

    import numpy as np

    out = dict(_drawn_inputs(seed))
    spreads = {'L0_gnn_ln_gamma': (1.0, 0.2), 'L0_gnn_ln_beta': (0.0, 0.1), 'L1_gnn_b': (0.0, 0.1)}
    factors = {'L0_gnn_diag_u': 8.0, 'L0_gnn_W_i': 5.56, 'L0_gnn_diag_i': 8.0}
    for name, (base, spread) in spreads.items():
        noise = np.random.default_rng([zlib.crc32(name.encode()), seed]).standard_normal(out[name].shape)
        drawn = base * np.exp(spread * noise) if base else spread * noise
        out[name] = jnp.asarray(drawn.astype(out[name].dtype))
    for name, factor in factors.items():
        out[name] = (out[name] * factor).astype(out[name].dtype)
    return out
```

```python
from contextlib import ExitStack

import concourse.bass as bass
from concourse import mybir

P = 128
F32 = mybir.dt.float32
BF16 = mybir.dt.bfloat16
I16 = mybir.dt.int16
FP8 = mybir.dt.float8e4
U8 = mybir.dt.uint8
ALU = mybir.AluOpType
ACT = mybir.ActivationFunctionType
AX_X = mybir.AxisListType.X
BANK = 512

LN_EPS = 1e-5
F_CONST, B_CONST, R_CONST = 1.0, 0.1, 0.01
MAX_NEIGH = 100
STEP = 128.0
W_UNIT = 2.0 ** (127 - MAX_NEIGH)


def resnorm_kernel(nc, x, adj, W_u, diag_u, par_u, W_i, diag_i, par_i, gamma, beta, W1, b1, W3, b3, out):
    N, F = x.shape
    K = N // P
    JP = 2
    PW = JP * P
    NP = N // PW
    KU = diag_u.shape[0] // P
    GK = 4
    NG = K // GK
    NS = K // 2
    BACK = 4
    SQRT_SLOT = 8
    P2_SLOT = NS // 2
    NB = 5
    KB = K // NB
    RW = KB * P
    MS = RW // PW
    assert N == NB * 2 * BANK and NS - P2_SLOT == NB * JP and NP % 2 == 0 and NP >= 4 and 2 * F == P

    x_d = x.rearrange("(k p) f -> p k f", p=P)
    out_d = out.rearrange("(k p) f -> p k f", p=P)
    adj_d = adj.rearrange("(k p) c -> p k c", p=P)
    mask_d = nc.dram_tensor("mask_t", [NP, NB, P, JP * RW], U8, kind="Internal").ap()

    ctx = ExitStack()
    with ctx:
        def sb(name, shape, dt=F32):
            return ctx.enter_context(nc.sbuf_tensor(name, shape, dt))

        def sem(name):
            return ctx.enter_context(nc.semaphore(name))

        xa = sb("xa", [P, K, F])
        xb = sb("xb", [P, K, F])
        ez = sb("ez", [P, K, F])
        at = [sb(f"at{i}", [P, JP, N]) for i in range(2)]
        nat = sb("nat", [P, K, PW])
        mask = nat[:, :, :].rearrange("p k c -> p (k c)").bitcast(FP8).rearrange("p (j r) -> p j r", j=K)
        hT = sb("hT", [P, NB * BANK])
        xT = sb("xT", [P, K // 2, P])
        hg = sb("hg", [P, KB, F])
        hs = sb("hs", [P, KB, F])
        tT = sb("tT", [P, PW])
        tv = [sb(f"tv{i}", [P, JP, F]) for i in range(2)]
        cy = sb("cy", [P, JP, F])
        cc = sb("cc", [P, JP, F])
        s_region = sb("s_region", [P, K * 3 * F], BF16)
        s12 = s_region[:, 0:K * 2 * F].rearrange("p (k c) -> p k c", k=K)
        s3 = s_region[:, K * 2 * F:K * 3 * F].rearrange("p (k c) -> p k c", k=K)
        mstage = [s_region[:, m * JP * RW // 2:(m + 1) * JP * RW // 2].bitcast(FP8) for m in range(NB)]
        wbits = [[sb(f"wbits{c}{i}", [P, BANK], I16) for i in range(2)] for c in range(2)]
        W2 = sb("W2", [P, 4, P])
        ident = sb("ident", [P, P])
        upto = sb("upto", [P, P], BF16)
        rest = sb("rest", [P, P], BF16)
        rows = sb("rows", [P, 4, F])
        par = sb("par", [P, 4])
        dg = sb("dg", [K, P])
        g = sb("g", [P, K])
        degp = sb("degp", [P, K, NB])
        dinv = sb("dinv", [P, K])
        sm = sb("sm", [P, 8, K])

        hacc = ctx.enter_context(nc.psum_tensor("hacc", [P, NB * BANK], F32))
        tacc = ctx.enter_context(nc.psum_tensor("tacc", [P, BANK], F32))
        turn = [ctx.enter_context(nc.psum_tensor(f"turn{i}", [P, BANK], F32)) for i in range(2)]

        in_small = sem("in_small")
        made_zero = sem("made_zero")
        consts = sem("consts")
        nat_in = [sem(f"nat_in{i}") for i in range(NG)]
        mask_in = [sem(f"mask_in{i}") for i in range(NB)]
        mask_out = [sem(f"mask_out{i}") for i in range(NB)]
        out_done = sem("out_done")
        nat_used = [sem(f"nat_used{s}") for s in range(2)]
        tr_done = [sem(f"tr_done{s}") for s in range(2)]
        at_ready = [sem(f"at_ready{s}") for s in range(2)]
        tT_ready = [sem(f"tT_ready{s}") for s in range(2)]
        back_done = [sem(f"back_done{s}") for s in range(2)]
        tv_ready = [sem(f"tv_ready{s}") for s in range(2)]
        back_read = [tv_ready[0], sem("back_read1")]
        p2_done = [sem(f"p2_done{s}") for s in range(2)]
        mask_made = sem("mask_made")
        var_ready = sem("var_ready")
        sd_ready = sem("sd_ready")
        chain = sem("chain")
        hT_ready = [sem(f"hT_ready{s}") for s in range(2)]
        h_back = [sem(f"h_back{s}") for s in range(2)]
        h_read = [sem(f"h_read{s}") for s in range(2)]
        x_ready = [sem(f"x_ready{s}") for s in range(3)]
        xt_done = [sem(f"xt_done{s}") for s in range(3)]
        xT_ready = [sem(f"xT_ready{s}") for s in range(3)]
        xw_done = [sem(f"xw_done{s}") for s in range(3)]
        v_ready = [sem(f"v_ready{s}") for s in range(3)]
        dg_done = sem("dg_done")
        cnt_done = sem("cnt_done")
        w_ready = sem("w_ready")
        w_used = sem("w_used")
        o_done = sem("o_done")
        oT_ready = sem("oT_ready")
        o_back = sem("o_back")
        o_read = sem("o_read")
        y_ready = sem("y_ready")

        passed = {nc.sync: sem("passed_sp"), nc.tensor: sem("passed_pe")}

        NVARS0, NVARS1 = 1 + 2 * NB, NP + NB

        block = ctx.enter_context(nc.Block())

        def wait_alone(eng, semaphore, value):
            eng.wait_ge(semaphore, value)
            eng.sem_inc(passed[eng], 1)

        @block.sync
        def _(sp):
            sp.dma_start(xa[:, :, :], x_d).then_inc(in_small, 16)
            sp.dma_start(dg[0:KU, :], diag_u.rearrange("(k p) -> k p", p=P)).then_inc(in_small, 16)
            sp.dma_start(dg[KU:K, :], diag_i.rearrange("(k p) -> k p", p=P)).then_inc(in_small, 16)
            for i, v in enumerate((par_u, par_i)):
                sp.dma_start(par[:, 2 * i:2 * i + 2], v.rearrange("(a n) -> a n", a=1).broadcast_to([P, 2])).then_inc(in_small, 16)
            for i, v in enumerate((gamma, beta, b1, b3)):
                sp.dma_start(rows[:, i, :], v.rearrange("(a n) -> a n", a=1).broadcast_to([P, F])).then_inc(in_small, 16)
            sp.wait_ge(made_zero, 1)
            for i, w in enumerate((W_u, W_i, W1, W3)):
                for h in range(2):
                    sp.dma_start(W2[h * F:(h + 1) * F, i, h * F:(h + 1) * F], w).then_inc(in_small, 16)

            def load(s, p, grp):
                sp.dma_start(nat[:, GK * grp:GK * (grp + 1), :],
                             adj_d[:, GK * grp:GK * (grp + 1), bass.ds(p * PW, PW)]).then_inc(nat_in[grp], 16)

            def panel_io(s, p, last):
                for m in range(NB):
                    if s == 0:
                        wait_alone(sp, mask_made, p * NB + m + 1)
                        sp.dma_start(mask_d[bass.ds(p, 1), m, :, :].rearrange("a p c -> p (a c)"), mstage[m].bitcast(U8)).then_inc(mask_out[m], 16)
                    if not last:
                        for grp in (2 * m, 2 * m + 1):
                            sp.wait_ge(nat_used[s], p * NG + grp + 1)
                            load(s, p + 1, grp)

            for s in range(2):
                for grp in range(NG):
                    if s == 1:
                        sp.wait_ge(nat_used[0], (NP - 1) * NG + grp + 1)
                    load(s, 0, grp)
                with sp.Fori(0, NP - 1) as p:
                    panel_io(s, p, False)
                panel_io(s, NP - 1, True)

            def load_mask(r, q):
                lo = NP - 4 * (q + 1)
                sp.dma_start(mask.bitcast(U8)[:, 2 * lo:2 * lo + 8, :].rearrange("p (n j) r -> p n (j r)", j=JP),
                             mask_d[lo:lo + 4, bass.ds(r, 1), :, :].rearrange("n a p c -> p (n a) c")).then_inc(mask_in[q], 16)

            sp.wait_ge(nat_used[1], NP * NG)
            for m in range(NB):
                sp.wait_ge(mask_out[m], 16 * NP)
            for q in range(NB):
                load_mask(0, q)
            with sp.Fori(1, NB) as r:
                for q in range(NB):
                    wait_alone(sp, w_used, (r - 1) * K + 8 * (q + 1))
                    load_mask(r, q)
            with sp.Fori(0, NB) as r:
                wait_alone(sp, y_ready, 2 * r + 2)
                sp.dma_start(out_d[:, bass.ds(r * KB, KB), :], xa[:, bass.ds(r * KB, KB), :]).then_inc(out_done, 16)
            sp.wait_ge(out_done, 16 * NB)

        @block.gpsimd
        def _(pool):
            pool.memset(W2[:, :, :], 0.0).then_inc(made_zero, 1)
            pool.memset(ident[:, :], 0.0).then_inc(consts, 1)
            pool.memset(upto[:, :], -STEP).then_inc(consts, 1)
            pool.memset(rest[:, :], -STEP).then_inc(consts, 1)
            pool.wait_ge(consts, 3)
            pool.affine_select(out=ident[:, :], in_=ident[:, :], compare_op=ALU.not_equal, fill=1.0,
                               base=0, pattern=[[-1, P]], channel_multiplier=1).then_inc(consts, 1)
            pool.affine_select(out=upto[:, :], in_=upto[:, :], compare_op=ALU.is_ge, fill=0.0,
                               base=0, pattern=[[-1, P]], channel_multiplier=1).then_inc(consts, 1)
            pool.affine_select(out=rest[:, :], in_=rest[:, :], compare_op=ALU.is_ge, fill=0.0,
                               base=0, pattern=[[1, P]], channel_multiplier=-1).then_inc(consts, 1)
            pool.wait_ge(consts, 6)
            pool.affine_select(out=upto[:, :], in_=upto[:, :], compare_op=ALU.not_equal, fill=STEP * MAX_NEIGH,
                               base=0, pattern=[[-1, P]], channel_multiplier=1).then_inc(consts, 1)
            pool.affine_select(out=rest[:, :], in_=rest[:, :], compare_op=ALU.not_equal,
                               fill=-STEP * (MAX_NEIGH + 1),
                               base=0, pattern=[[-1, P]], channel_multiplier=1).then_inc(consts, 1)

        @block.tensor
        def _(pe):
            mm = nc.tensor.matmul

            def turned(dst, src):
                return mm(dst, src, ident[0:src.shape[0], 0:src.shape[0]], start=True, stop=True, is_transpose=True)

            def project(n, src, weight_of, ahead=None):
                for b in range(NB):
                    if ahead and b + 2 < NB:
                        ahead(b + 2)
                    pe.wait_ge(x_ready[n], b + 1)
                    for q in range(KB // 2):
                        k = b * KB + 2 * q
                        last = turned(tacc[:, q * P:(q + 1) * P],
                                      src[:, k:k + 2, :].rearrange("p k f -> p (k f)"))
                    last.then_inc(xt_done[n], 1)
                    pe.wait_ge(xT_ready[n], b + 1)
                    for q in range(KB // 2):
                        last = mm(hacc[:, b * BANK + q * P:b * BANK + (q + 1) * P], xT[:, b * KB // 2 + q, :],
                                  W2[:, weight_of(b * KB), :], start=True, stop=True)
                    last.then_inc(xw_done[n], 1)

            def first_product(s, p, k):
                h = k % 2
                return mm(tacc[h * F:(h + 1) * F, 0:PW], ez[:, k, :], nat[:, k, :],
                          start=(k < 2), stop=(k >= K - 2), skip_group_check=True)

            def second_product(s, p, n, first, last_panel=False):
                c, j = n // JP, n % JP
                for h in range(2):
                    last = mm(hacc[h * F:(h + 1) * F, c * BANK:(c + 1) * BANK], tv[p % 2][:, j, :],
                              at[p % 2][:, j, (2 * c + h) * BANK:(2 * c + h + 1) * BANK],
                              start=(first and j == 0), stop=(last_panel and j == JP - 1), skip_group_check=True)
                if n == NB * JP - 1:
                    last.then_inc(p2_done[s], 1)

            def back(s, p, par_):
                pe.wait_ge(tT_ready[s], p)
                for j in range(JP):
                    last = turned(turn[(par_ + BACK) % 2][:, j * P:(j + 1) * P], tT[:, j * P:(j + 1) * P])
                last.then_inc(back_done[s], 1)

            def panel(s, p, par_, first, second_first):
                for q in range(NS):
                    idx = q + (q >= BACK)
                    if q == BACK and not first:
                        pe.wait_ge(at_ready[s], p * NS + BACK - 2 + 1)
                        back(s, p, par_)
                    if idx == BACK + 2 and not first:
                        pe.wait_ge(back_read[s], p)
                    elif idx == BACK + 2:
                        pe.wait_ge(at_ready[s], BACK - 2 + 1)
                    elif not (first and q < 2):
                        prev = p * NS + (q - 2 if q < BACK or q > BACK + 1 else q - 1)
                        pe.wait_ge(at_ready[s], prev + 1)
                    if q % 2 == 0:
                        pe.wait_ge(nat_in[q // 2], 16 * (p + 1 + s * NP))
                    bank = turn[(par_ + idx) % 2]
                    for kk in range(2):
                        for j in range(JP):
                            last = turned(bank[:, j * PW + kk * P:j * PW + (kk + 1) * P],
                                          nat[:, 2 * q + kk, j * P:(j + 1) * P])
                    last.then_inc(tr_done[s], 1)
                    if q == 0 and not first:
                        pe.wait_ge(tT_ready[s], p)
                    for kk in range(2):
                        last = first_product(s, p, 2 * q + kk)
                    if q % 2 == 1:
                        last.then_inc(nat_used[s], 1)
                    if q == P2_SLOT and not first:
                        pe.wait_ge(tv_ready[s], p)
                    if q >= P2_SLOT and not first:
                        second_product(s, (par_ + 1) % 2, q - P2_SLOT, second_first)

            def sweep(s):
                panel(s, 0, 0, True, False)
                panel(s, 1, 1, False, True)
                with pe.Fori(1, NP // 2) as h:
                    panel(s, 2 * h, 0, False, False)
                    panel(s, 2 * h + 1, 1, False, False)
                pe.wait_ge(at_ready[s], NP * NS)
                back(s, NP, 0)
                pe.wait_ge(tv_ready[s], NP)
                for n in range(NB * JP):
                    second_product(s, 1, n, False, True)
                def turn_group(b):
                    pe.wait_ge(hT_ready[s], b + 1)
                    if b >= 2:
                        pe.wait_ge(h_read[s], b - 1)
                    for q in range(4):
                        last = turned(turn[b % 2][:, q * P:(q + 1) * P], hT[:, b * BANK + q * P:b * BANK + (q + 1) * P])
                    last.then_inc(h_back[s], 1)

                turn_group(0)
                turn_group(1)
                project(s + 1, xb, lambda k: s + 2, turn_group)

            pe.wait_ge(in_small, 16 * 17)
            pe.wait_ge(consts, 8)
            turned(tacc[:, 0:K], dg[:, :]).then_inc(dg_done, 1)
            project(0, xa, lambda k: 0 if k < KU else 1)
            pe.wait_ge(v_ready[0], NB)
            sweep(0)
            pe.wait_ge(v_ready[1], NB)
            sweep(1)
            pe.wait_ge(v_ready[2], NB)

            cnt = [hacc[:, c * BANK:(c + 1) * BANK] for c in range(2)]
            acc = [hacc[:, (2 + c) * BANK:(3 + c) * BANK] for c in range(2)]

            def weigh(r, n):
                j = K - 1 - n
                pe.wait_ge(w_ready, (r * K + n) * 2 + 2)
                for c in range(2):
                    mm(acc[c], s12[:, j, :], wbits[c][n % 2][:, :].bitcast(BF16), start=(n == 0), stop=False,
                       skip_group_check=True)
                for c in range(2):
                    last = mm(acc[c][c * F:(c + 1) * F, :], s3[:, j, :], wbits[c][n % 2][:, :].bitcast(BF16),
                              start=False, stop=(n == K - 1), skip_group_check=True)
                last.then_inc(w_used, 1)

            with pe.Fori(0, NB) as r:
                for n in range(K):
                    j = K - 1 - n
                    if n % 8 == 0:
                        wait_alone(pe, mask_in[n // 8], r * 16 + 16)
                    for c in range(2):
                        mm(cnt[c], upto[:, :], mask[:, j, c * BANK:(c + 1) * BANK], start=(n == 0),
                           stop=False, skip_group_check=True).then_inc(cnt_done, 1)
                    if n > 0:
                        weigh(r, n - 1)
                    if n < K - 1:
                        if n == 0:
                            wait_alone(pe, w_ready, r * K * 2 + 2)
                        for c in range(2):
                            if n > 0:
                                wait_alone(pe, w_ready, (r * K + n) * 2 + c + 1)
                            mm(cnt[c], rest[:, :], mask[:, j, c * BANK:(c + 1) * BANK], start=False,
                               stop=False, skip_group_check=True)
                weigh(r, K - 1)
                for c in range(2):
                    pe.wait_ge(oT_ready, r * 2 + c + 1)
                    for q in range(4):
                        last = turned(turn[c][:, q * P:(q + 1) * P], hT[:, c * BANK + q * P:c * BANK + (q + 1) * P])
                    last.then_inc(o_back, 1)

        @block.scalar
        def _(act):
            copy = ACT.Copy

            def root(i, n):
                act.wait_ge(var_ready, i + 1)
                nc.scalar.activation(sm[:, 3, 0:n], sm[:, 2, 0:n], ACT.Sqrt).then_inc(sd_ready, 1)

            def project(n, b):
                act.wait_ge(xt_done[n], b + 1)
                nc.scalar.activation(xT[:, b * KB // 2:(b + 1) * KB // 2, :].rearrange("p q i -> p (q i)"),
                                     tacc[:, :], copy).then_inc(xT_ready[n], 1)

            def panel(s, p, par_, first, reused):
                for q in range(NS):
                    idx = q + (q >= BACK)
                    if q == 0 and reused and s == 0:
                        act.wait_ge(mask_made, (p - 1) * NB)
                    act.wait_ge(tr_done[s], p * NS + q + 1)
                    nc.scalar.activation(at[par_][:, :, q * PW:(q + 1) * PW],
                                         turn[(par_ + idx) % 2][:, :].rearrange("p (j c) -> p j c", j=JP),
                                         copy).then_inc(at_ready[s], 1)
                    if q == SQRT_SLOT and s == 1 and not first:
                        root(NVARS0 + p - 1, JP)

            for b in range(NB):
                project(0, b)
            for s in range(2):
                if s == 1:
                    act.wait_ge(mask_made, NP * NB)
                panel(s, 0, 0, True, False)
                panel(s, 1, 1, False, False)
                with act.Fori(1, NP // 2) as h:
                    panel(s, 2 * h, 0, False, True)
                    panel(s, 2 * h + 1, 1, False, True)
                if s == 1:
                    root(NVARS0 + NP - 1, JP)
                act.wait_ge(p2_done[s], NP)
                for b in range(NB):
                    nc.scalar.activation(hT[:, b * BANK:(b + 1) * BANK], hacc[:, b * BANK:(b + 1) * BANK],
                                         copy).then_inc(hT_ready[s], 1)
                if s == 0:
                    root(0, K)
                for b in range(NB):
                    if s == 0:
                        root(1 + 2 * b, KB)
                        root(2 + 2 * b, KB)
                    else:
                        root(NVARS0 + NP + b, KB)
                    project(s + 1, b)

            with act.Fori(0, NB) as r:
                for n in range(K):
                    for c in range(2):
                        act.wait_ge(cnt_done, (r * K + n) * 2 + c + 1)
                        if n >= 2:
                            act.wait_ge(w_used, r * K + n - 1)
                        nc.scalar.activation(wbits[c][n % 2][:, :], hacc[:, c * BANK:(c + 1) * BANK], ACT.Relu).then_inc(w_ready, 1)
                for c in range(2):
                    root(NVARS0 + NVARS1 + 2 * r + c, 4)

        @block.vector
        def _(dve):
            V = nc.vector
            done = [0]

            def link(ins):
                done[0] = done[0] + 1
                ins.then_inc(chain, 1)
                dve.wait_ge(chain, done[0])

            def over_f(col, n):
                return col.rearrange("p (n a) -> p n a", a=1).broadcast_to([P, n, F])

            def over_n(row, n):
                return row.rearrange("p (a f) -> p a f", a=1).broadcast_to([P, n, F])

            def inverse_root(i, n):
                v, sd, r0, u = (sm[:, c, 0:n] for c in (2, 3, 4, 5))
                dve.wait_ge(sd_ready, i + 1)
                link(V.reciprocal(r0, sd))
                link(V.tensor_tensor(u, r0, r0, ALU.mult))
                link(V.tensor_tensor(u, u, v, ALU.mult))
                link(V.tensor_scalar(u, u, -0.5, 1.5, ALU.mult, ALU.add))
                link(V.tensor_tensor(u, u, r0, ALU.mult))
                return u

            def layer_norm(dst, src, tmp, i, n):
                mean, ss, var = sm[:, 0, 0:n], sm[:, 1, 0:n], sm[:, 2, 0:n]
                link(V.tensor_reduce(mean, src, AX_X, ALU.add))
                link(V.tensor_scalar(mean, mean, 1.0 / F, None, ALU.mult))
                link(V.tensor_tensor(src, src, over_f(mean, n), ALU.subtract))
                link(V.tensor_tensor(tmp, src, src, ALU.mult))
                link(V.tensor_reduce(ss, tmp, AX_X, ALU.add))
                V.tensor_scalar(var, ss, 1.0 / F, LN_EPS, ALU.mult, ALU.add).then_inc(var_ready, 1)
                r = inverse_root(i, n)
                return V.tensor_tensor(dst, src, over_f(r, n), ALU.mult)

            dve.wait_ge(in_small, 16 * 17)
            link(V.tensor_tensor(sm[:, 6, 0:1], par[:, 0:1], par[:, 1:2], ALU.mult))
            link(V.tensor_tensor(sm[:, 6, 1:2], par[:, 2:3], par[:, 3:4], ALU.mult))
            dve.wait_ge(dg_done, 1)
            link(V.tensor_scalar(g[:, 0:KU], tacc[:, 0:KU], sm[:, 6, 0:1], None, ALU.mult))
            V.tensor_scalar(g[:, KU:K], tacc[:, KU:K], sm[:, 6, 1:2], None, ALU.mult).then_inc(x_ready[0], NB)
            dve.wait_ge(x_ready[0], NB)

            def group(t, b):
                return t[:, b * KB:(b + 1) * KB, :]

            def bank(b):
                return hacc[:, b * BANK:(b + 1) * BANK].rearrange("p (n f) -> p n f", n=KB)

            for b in range(NB):
                dve.wait_ge(xw_done[0], b + 1)
                link(V.tensor_tensor(hg[:, :, :], bank(b), over_f(g[:, b * KB:(b + 1) * KB], KB), ALU.mult))
                V.tensor_tensor(group(ez, b), hg[:, :, :], group(xa, b), ALU.add).then_inc(v_ready[0], 1)
                dve.wait_ge(v_ready[0], b + 1)

            def take(s, p):
                dve.wait_ge(nat_used[s], (p + 1) * NG)
                return V.tensor_copy(tT[:, :], tacc[:, 0:PW]).then_inc(tT_ready[s], 1)

            def halves(par_):
                return turn[(par_ + BACK) % 2][:, 0:PW].rearrange("p (j h f) -> p j f h", j=JP, h=2)

            def masks(p, par_, m, first):
                rows_ = slice(m * RW, (m + 1) * RW)
                dve.wait_ge(at_ready[0], p * NS + MS * (m + 1))
                if not first:
                    dve.wait_ge(mask_out[m], p * 16)
                V.tensor_reduce(degp[:, bass.ds(p * JP, JP), m], at[par_][:, :, rows_], AX_X, ALU.add)
                V.tensor_scalar(mstage[m].rearrange("p (j r) -> p j r", j=JP), at[par_][:, :, rows_], 0.0, None,
                                ALU.not_equal, saturate=False).then_inc(mask_made, 1)

            def panel0(p, par_, first):
                if not first:
                    dve.wait_ge(back_done[0], p)
                    V.tensor_reduce(tv[1 - par_][:, :, :], halves(par_), AX_X, ALU.add).then_inc(tv_ready[0], 1)
                for m in range(NB - 1):
                    masks(p, par_, m, first)
                take(0, p)
                masks(p, par_, NB - 1, first)

            panel0(0, 0, True)
            panel0(1, 1, False)
            with dve.Fori(1, NP // 2) as h:
                panel0(2 * h, 0, False)
                panel0(2 * h + 1, 1, False)
            dve.wait_ge(back_done[0], NP)
            V.tensor_reduce(tv[1][:, :, :], halves(0), AX_X, ALU.add).then_inc(tv_ready[0], 1)

            dve.wait_ge(mask_made, NP * NB)
            link(V.tensor_reduce(sm[:, 0, :], degp[:, :, :], AX_X, ALU.add))
            link(V.tensor_scalar(sm[:, 0, :], sm[:, 0, :], 1.0, None, ALU.add))
            link(V.tensor_scalar(sm[:, 1, :], sm[:, 0, :], 0.0, None, ALU.is_gt))
            V.tensor_scalar(sm[:, 2, :], sm[:, 0, :], 2.0 ** -100, None, ALU.max).then_inc(var_ready, 1)
            r = inverse_root(0, K)
            link(V.tensor_tensor(dinv[:, :], r, sm[:, 1, :], ALU.mult))

            def turned_group(s, b):
                dve.wait_ge(h_back[s], b + 1)
                return turn[b % 2][:, :].rearrange("p (q h f) -> p h q f", q=4, h=2)

            def by_half(t):
                return t.rearrange("p (h q) f -> p h q f", h=2)

            def finish_z(b):
                dve.wait_ge(xw_done[1], b + 1)
                V.tensor_tensor(group(ez, b), bank(b), over_f(dinv[:, b * KB:(b + 1) * KB], KB),
                                ALU.mult).then_inc(v_ready[1], 1)

            for b in range(NB):
                src = turned_group(0, b)
                ins = V.tensor_copy(by_half(hg[:, :, :]), src)
                ins.then_inc(h_read[0], 1)
                dve.wait_ge(h_read[0], b + 1)
                link(layer_norm(hg[:, :, :], hg[:, :, :], hs[:, :, :], 1 + 2 * b, KB))
                link(V.tensor_tensor(hg[:, :, :], hg[:, :, :], over_n(rows[:, 0, :], KB), ALU.mult))
                link(V.tensor_tensor(hg[:, :, :], hg[:, :, :], over_n(rows[:, 1, :], KB), ALU.add))
                link(V.scalar_tensor_tensor(hg[:, :, :], group(xa, b), 2.0, hg[:, :, :], ALU.mult, ALU.add))
                layer_norm(group(xb, b), hg[:, :, :], hs[:, :, :], 2 + 2 * b, KB).then_inc(x_ready[1], 1)
                dve.wait_ge(x_ready[1], b + 1)
                if b:
                    finish_z(b - 1)
            finish_z(NB - 1)

            def x2_of(p, par_):
                dve.wait_ge(back_done[1], p)
                blk = bass.ds((p - 1) * JP, JP)
                V.tensor_reduce(cy[:, :, :], halves(par_), AX_X, ALU.add).then_inc(back_read[1], 1)
                dve.wait_ge(back_read[1], p)
                link(V.tensor_tensor(cy[:, :, :], cy[:, :, :], ez[:, blk, :], ALU.add))
                link(V.tensor_tensor(cy[:, :, :], cy[:, :, :], over_f(dinv[:, blk], JP), ALU.mult))
                link(V.tensor_tensor(cy[:, :, :], cy[:, :, :], over_n(rows[:, 2, :], JP), ALU.add))
                link(V.scalar_tensor_tensor(cy[:, :, :], cy[:, :, :], 0.0, xb[:, blk, :], ALU.max, ALU.add))
                dst = tv[1 - par_][:, :, :]
                layer_norm(dst, cy[:, :, :], cc[:, :, :], NVARS0 + p - 1, JP).then_inc(tv_ready[1], 1)
                dve.wait_ge(tv_ready[1], p)
                link(V.tensor_copy(xa[:, blk, :], dst))

            X2_LINKS = 4 + 5 + 5 + 1

            def panel1(p, par_, first):
                if not first:
                    x2_of(p, par_)
                take(1, p)

            panel1(0, 0, True)
            panel1(1, 1, False)
            before = done[0]
            with dve.Fori(1, NP // 2) as h:
                done[0] = before + (2 * h - 2) * X2_LINKS
                panel1(2 * h, 0, False)
                panel1(2 * h + 1, 1, False)
            done[0] = before + (NP - 2) * X2_LINKS
            x2_of(NP, 0)

            def finish_s(b):
                dve.wait_ge(xw_done[2], b + 1)
                link(V.tensor_scalar(hs[:, :, :], bank(b), W_UNIT, None, ALU.mult))
                s1, s2 = group(s12, b)[:, :, 0:F], group(s12, b)[:, :, F:2 * F]
                link(V.tensor_copy(s1, hs[:, :, :]))
                link(V.tensor_tensor(hs[:, :, :], hs[:, :, :], s1, ALU.subtract))
                link(V.tensor_copy(s2, hs[:, :, :]))
                V.tensor_tensor(group(s3, b), hs[:, :, :], s2, ALU.subtract).then_inc(v_ready[2], 1)
                dve.wait_ge(v_ready[2], b + 1)

            for m in range(NB):
                dve.wait_ge(mask_out[m], 16 * NP)
            for b in range(NB):
                src = turned_group(1, b)
                V.tensor_tensor(by_half(hg[:, :, :]), src, by_half(group(xa, b)), ALU.mult).then_inc(h_read[1], 1)
                dve.wait_ge(h_read[1], b + 1)
                link(V.tensor_reduce(sm[:, 6, 0:KB], hg[:, :, :], AX_X, ALU.add))
                link(V.tensor_scalar(sm[:, 6, 0:KB], sm[:, 6, 0:KB], R_CONST, None, ALU.mult))
                link(V.tensor_scalar(hg[:, :, :], group(xa, b), -B_CONST, F_CONST, ALU.mult, ALU.add))
                link(V.tensor_tensor(hg[:, :, :], hg[:, :, :], over_f(sm[:, 6, 0:KB], KB), ALU.subtract))
                link(V.tensor_tensor(hg[:, :, :], hg[:, :, :], group(xa, b), ALU.add))
                layer_norm(group(xb, b), hg[:, :, :], hs[:, :, :], NVARS0 + NP + b, KB).then_inc(x_ready[2], 1)
                dve.wait_ge(x_ready[2], b + 1)
                if b:
                    finish_s(b - 1)
            finish_s(NB - 1)

            O_LINKS = 3 + 5 + 5
            before = done[0]
            HK = KB // 2
            with dve.Fori(0, NB) as r:
                done[0] = before + r * (2 * O_LINKS)
                dve.wait_ge(w_used, r * K + K)
                for c in range(2):
                    V.tensor_copy(hT[:, c * BANK:(c + 1) * BANK], hacc[:, (2 + c) * BANK:(3 + c) * BANK]).then_inc(oT_ready, 1)
                for c in range(2):
                    blk = bass.ds(r * KB + c * HK, HK)
                    o = hg[:, c * HK:(c + 1) * HK, :]
                    dve.wait_ge(o_back, r * 2 + c + 1)
                    link(V.tensor_reduce(o, turn[c][:, :].rearrange("p (q h f) -> p q f h", q=4, h=2), AX_X, ALU.add))
                    link(V.tensor_tensor(o, o, over_n(rows[:, 3, :], HK), ALU.add))
                    link(V.tensor_tensor(o, o, xb[:, blk, :], ALU.add))
                    layer_norm(xa[:, blk, :], o, hs[:, 0:HK, :], NVARS0 + NVARS1 + r * 2 + c, HK).then_inc(y_ready, 1)
                    dve.wait_ge(y_ready, r * 2 + c + 1)


_INS = ['x', 'adj', 'L0_gnn_W_u', 'L0_gnn_diag_u', 'L0_gnn_par_u', 'L0_gnn_W_i', 'L0_gnn_diag_i', 'L0_gnn_par_i',
        'L0_gnn_ln_gamma', 'L0_gnn_ln_beta', 'L1_gnn_W', 'L1_gnn_b', 'L3_gnn_weight', 'L3_gnn_bias']


def kernel(**inputs):
    import numpy as _np
    import concourse.bacc as _bacc
    from concourse import mybir as _mybir
    from concourse.bass_utils import run_bass_kernel_spmd as _run

    nc = _bacc.Bacc("TRN2", target_bir_lowering=False, num_devices=1)
    arrays, args = {}, []
    for name in _INS:
        a = _np.ascontiguousarray(inputs[name])
        arrays[f"in_{name}"] = a
        args.append(nc.dram_tensor(f"in_{name}", a.shape, _mybir.dt.from_np(a.dtype), kind="ExternalInput").ap())
    shape = inputs['x'].shape
    args.append(nc.dram_tensor("out_x", shape, F32, kind="ExternalOutput").ap())
    resnorm_kernel(nc, *args)
    r = _run(nc, [arrays], core_ids=[0])
    return r.results[0]["out_x"]
```

```python
from contextlib import ExitStack

import concourse.bass as bass
from concourse import mybir

P = 128
F32 = mybir.dt.float32
F32R = mybir.dt.float32r
BF16 = mybir.dt.bfloat16
I16 = mybir.dt.int16
FP8 = mybir.dt.float8e4
U8 = mybir.dt.uint8
ALU = mybir.AluOpType
ACT = mybir.ActivationFunctionType
AX_X = mybir.AxisListType.X
BANK = 512

LN_EPS = 1e-5
F_CONST, B_CONST, R_CONST = 1.0, 0.1, 0.01
MAX_NEIGH = 100
STEP = 128.0
W_UNIT = 2.0 ** (127 - MAX_NEIGH)


def resnorm_kernel(nc, x, adj, W_u, diag_u, par_u, W_i, diag_i, par_i, gamma, beta, W1, b1, W3, b3, out):
    N, F = x.shape
    K = N // P
    JP = 2
    PW = JP * P
    NP = N // PW
    KU = diag_u.shape[0] // P
    GK = 4
    NG = K // GK
    NS = K // 2
    BACK = 4
    SQRT_SLOT = 8
    P2_SLOT = NS // 2
    NB = 5
    KB = K // NB
    RW = KB * P
    MS = RW // PW
    assert N == NB * 2 * BANK and NS - P2_SLOT == NB * JP and NP % 2 == 0 and NP >= 4 and 2 * F == P

    x_d = x.rearrange("(k p) f -> p k f", p=P)
    out_d = out.rearrange("(k p) f -> p k f", p=P)
    adj_d = adj.rearrange("(k p) c -> p k c", p=P)
    mask_d = nc.dram_tensor("mask_t", [NP, NB, P, JP * RW], U8, kind="Internal").ap()

    ctx = ExitStack()
    with ctx:
        def sb(name, shape, dt=F32):
            return ctx.enter_context(nc.sbuf_tensor(name, shape, dt))

        def sem(name):
            return ctx.enter_context(nc.semaphore(name))

        xa = sb("xa", [P, K, F])
        xb = sb("xb", [P, K, F])
        ez = sb("ez", [P, K, F])
        at = [sb(f"at{i}", [P, JP, N]) for i in range(2)]
        nat = sb("nat", [P, K, PW])
        mask = nat[:, :, :].rearrange("p k c -> p (k c)").bitcast(FP8).rearrange("p (j r) -> p j r", j=K)
        hT = sb("hT", [P, NB * BANK])
        mstage = [hT[:, m * BANK:(m + 1) * BANK].bitcast(FP8) for m in range(NB)]
        xT = [sb(f"xT{i}", [P, KB // 2, P]) for i in range(2)]
        hg = [sb(f"hg{i}", [P, KB, F]) for i in range(2)]
        junk = sb("junk", [P, KB, F])
        cy, cc = junk[:, 0:JP, :], junk[:, JP:2 * JP, :]
        tT = sb("tT", [P, PW])
        tv = [sb(f"tv{i}", [P, JP, F]) for i in range(2)]
        s2 = sb("s2", [P, K, 2 * F], F32R)
        wr = [[sb(f"wr{c}{i}", [P, BANK], F32R) for i in range(2)] for c in range(2)]
        wbits = [[at[0][:, 0, (2 * c + i) * BANK:(2 * c + i) * BANK + BANK // 2].bitcast(I16) for i in range(2)]
                 for c in range(2)]
        W2 = sb("W2", [P, 4, P])
        ident = sb("ident", [P, P])
        center = sb("center", [P, P])
        centerg = sb("centerg", [P, P])
        upto = sb("upto", [P, P], BF16)
        rest = sb("rest", [P, P], BF16)
        rows = sb("rows", [P, 4, F])
        par = sb("par", [P, 4])
        dg = sb("dg", [K, P])
        g = sb("g", [P, K])
        degp = sb("degp", [P, K, NB])
        dinv = sb("dinv", [P, K])
        sm = sb("sm", [P, 7, K])

        hacc = ctx.enter_context(nc.psum_tensor("hacc", [P, NB * BANK], F32))
        tacc = ctx.enter_context(nc.psum_tensor("tacc", [P, BANK], F32))
        turn = [ctx.enter_context(nc.psum_tensor(f"turn{i}", [P, BANK], F32)) for i in range(2)]

        in_small = sem("in_small")
        made_zero = sem("made_zero")
        consts = sem("consts")
        nat_in = [sem(f"nat_in{i}") for i in range(NG)]
        mask_in = [sem(f"mask_in{i}") for i in range(NB)]
        mask_out = [sem(f"mask_out{i}") for i in range(NB)]
        out_done = sem("out_done")
        nat_used = [sem(f"nat_used{s}") for s in range(2)]
        tr_done = [sem(f"tr_done{s}") for s in range(2)]
        at_ready = [sem(f"at_ready{s}") for s in range(2)]
        tT_ready = [sem(f"tT_ready{s}") for s in range(2)]
        back_done = [sem(f"back_done{s}") for s in range(2)]
        tv_ready = [sem(f"tv_ready{s}") for s in range(2)]
        back_read = [tv_ready[0], sem("back_read1")]
        mask_made = sem("mask_made")
        u_ready = sem("u_ready")
        xb3_ready = sem("xb3_ready")
        cen_ready = sem("cen_ready")
        sq_ready = sem("sq_ready")
        bank_done = [sem(f"bank_done{s}") for s in range(2)]
        var_ready = sem("var_ready")
        sd_ready = sem("sd_ready")
        chain = sem("chain")
        hT_ready = [sem(f"hT_ready{s}") for s in range(2)]
        h_back = [sem(f"h_back{s}") for s in range(2)]
        h_read = sem("h_read")
        hg_back = sem("hg_back")
        centerg_ready = sem("centerg_ready")
        x_ready = [sem(f"x_ready{s}") for s in range(3)]
        xt_done = [sem(f"xt_done{s}") for s in range(3)]
        xT_ready = [sem(f"xT_ready{s}") for s in range(3)]
        xw_done = [sem(f"xw_done{s}") for s in range(3)]
        v_ready = [sem(f"v_ready{s}") for s in range(3)]
        dg_done = sem("dg_done")
        cnt_done = sem("cnt_done")
        bits_ready = sem("bits_ready")
        w_ready = sem("w_ready")
        w_used = sem("w_used")
        oT_ready = [sem(f"oT_ready{c}") for c in range(2)]
        o_back = sem("o_back")
        y_ready = sem("y_ready")

        passed = {nc.sync: sem("passed_sp"), nc.tensor: sem("passed_pe")}

        NVARS0, NVARS1 = 1 + NB + 1, NP + NB

        cnt = [hacc[:, b * BANK:(b + 1) * BANK] for b in (4, 3)]
        acc = [hacc[:, b * BANK:(b + 1) * BANK] for b in (2, 1)]
        FINISH, FSTEPS, FROOT = 4, 8, 5

        def order(s):
            return list(range(NB)) if s == 0 else list(range(NB - 1, -1, -1))

        block = ctx.enter_context(nc.Block())

        def wait_alone(eng, semaphore, value):
            eng.wait_ge(semaphore, value)
            eng.sem_inc(passed[eng], 1)

        @block.sync
        def _(sp):
            sp.dma_start(xa[:, :, :], x_d).then_inc(in_small, 16)
            sp.dma_start(dg[0:KU, :], diag_u.rearrange("(k p) -> k p", p=P)).then_inc(in_small, 16)
            sp.dma_start(dg[KU:K, :], diag_i.rearrange("(k p) -> k p", p=P)).then_inc(in_small, 16)
            for i, v in enumerate((par_u, par_i)):
                sp.dma_start(par[:, 2 * i:2 * i + 2], v.rearrange("(a n) -> a n", a=1).broadcast_to([P, 2])).then_inc(in_small, 16)
            for i, v in enumerate((gamma, beta, b1, b3)):
                sp.dma_start(rows[:, i, :], v.rearrange("(a n) -> a n", a=1).broadcast_to([P, F])).then_inc(in_small, 16)
            sp.wait_ge(made_zero, 1)
            for i, w in enumerate((W_u, W_i, W1, W3)):
                for h in range(2):
                    sp.dma_start(W2[h * F:(h + 1) * F, i, h * F:(h + 1) * F], w).then_inc(in_small, 16)

            def load(column, grp):
                sp.dma_start(nat[:, GK * grp:GK * (grp + 1), :],
                             adj_d[:, GK * grp:GK * (grp + 1), bass.ds(column, PW)]).then_inc(nat_in[grp], 16)

            def store_mask(p, m):
                sp.dma_start(mask_d[bass.ds(p, 1), m, :, :].rearrange("a p c -> p (a c)"),
                             mstage[m].bitcast(U8)).then_inc(mask_out[m], 16)

            def load_group(s, p, grp, column):
                sp.wait_ge(nat_used[s], p * NG + grp + 1)
                load(column, grp)

            for grp in range(NG):
                load(0, grp)
            with sp.Fori(0, NP - 1) as p:
                for m in range(NB):
                    wait_alone(sp, mask_made, p * NB + m + 1)
                    store_mask(p, m)
                    for grp in (2 * m, 2 * m + 1):
                        load_group(0, p, grp, (p + 1) * PW)
            for m in range(NB):
                sp.wait_ge(mask_made, (NP - 1) * NB + m + 1)
                store_mask(NP - 1, m)

            for grp in range(NG):
                load_group(1, 0, grp, (NP - 2) * PW)
            with sp.Fori(1, NP - 1) as p:
                for grp in range(NG):
                    load_group(1, p, grp, (p - 1) * PW)

            def load_mask(r, q):
                lo = NP - 4 * (q + 1)
                sp.dma_start(mask.bitcast(U8)[:, 2 * lo:2 * lo + 8, :].rearrange("p (n j) r -> p n (j r)", j=JP),
                             mask_d[lo:lo + 4, bass.ds(r, 1), :, :].rearrange("n a p c -> p (n a) c")).then_inc(mask_in[q], 16)

            sp.wait_ge(nat_used[1], NP * NG)
            for m in range(NB):
                sp.wait_ge(mask_out[m], 16 * NP)
            for q in range(NB):
                load_mask(0, q)
            with sp.Fori(1, NB) as r:
                for q in range(NB):
                    wait_alone(sp, w_used, (r - 1) * K + 8 * (q + 1))
                    load_mask(r, q)
            with sp.Fori(0, NB) as r:
                wait_alone(sp, y_ready, 2 * r + 2)
                sp.dma_start(out_d[:, bass.ds(r * KB, KB), :], xa[:, bass.ds(r * KB, KB), :]).then_inc(out_done, 16)
            sp.wait_ge(out_done, 16 * NB)

        @block.gpsimd
        def _(pool):
            pool.memset(W2[:, :, :], 0.0).then_inc(made_zero, 1)
            pool.memset(ident[:, :], 0.0).then_inc(consts, 1)
            pool.memset(center[:, :], -1.0 / F).then_inc(consts, 1)
            pool.memset(upto[:, :], -STEP).then_inc(consts, 1)
            pool.memset(rest[:, :], -STEP).then_inc(consts, 1)
            pool.wait_ge(consts, 4)
            pool.affine_select(out=ident[:, :], in_=ident[:, :], compare_op=ALU.not_equal, fill=1.0,
                               base=0, pattern=[[-1, P]], channel_multiplier=1).then_inc(consts, 1)
            pool.affine_select(out=upto[:, :], in_=upto[:, :], compare_op=ALU.is_ge, fill=0.0,
                               base=0, pattern=[[-1, P]], channel_multiplier=1).then_inc(consts, 1)
            pool.affine_select(out=rest[:, :], in_=rest[:, :], compare_op=ALU.is_ge, fill=0.0,
                               base=0, pattern=[[1, P]], channel_multiplier=-1).then_inc(consts, 1)
            pool.wait_ge(consts, 7)
            pool.memset(center[0:F, F:P], 0.0).then_inc(consts, 1)
            pool.memset(center[F:P, 0:F], 0.0).then_inc(consts, 1)
            pool.wait_ge(consts, 9)
            pool.affine_select(out=center[:, :], in_=center[:, :], compare_op=ALU.not_equal, fill=1.0 - 1.0 / F,
                               base=0, pattern=[[-1, P]], channel_multiplier=1).then_inc(consts, 1)
            pool.affine_select(out=upto[:, :], in_=upto[:, :], compare_op=ALU.not_equal, fill=STEP * MAX_NEIGH,
                               base=0, pattern=[[-1, P]], channel_multiplier=1).then_inc(consts, 1)
            pool.affine_select(out=rest[:, :], in_=rest[:, :], compare_op=ALU.not_equal,
                               fill=-STEP * (MAX_NEIGH + 1),
                               base=0, pattern=[[-1, P]], channel_multiplier=1).then_inc(consts, 1)
            pool.wait_ge(x_ready[0], NB)
            pool.tensor_scalar(xb[:, :, :], xa[:, :, :], 2.0, None, ALU.mult).then_inc(u_ready, 1)
            pool.wait_ge(u_ready, 1)
            pool.tensor_tensor(xb[:, :, :], xb[:, :, :],
                               rows[:, 1, :].rearrange("p (a f) -> p a f", a=1).broadcast_to([P, K, F]),
                               ALU.add).then_inc(u_ready, 1)
            pool.wait_ge(xt_done[2], NB)
            pool.tensor_tensor(xb[:, :, :], xb[:, :, :],
                               rows[:, 3, :].rearrange("p (a f) -> p a f", a=1).broadcast_to([P, K, F]),
                               ALU.add).then_inc(xb3_ready, 1)

        @block.tensor
        def _(pe):
            mm = nc.tensor.matmul

            def turned(dst, src):
                return mm(dst, src, ident[0:src.shape[0], 0:src.shape[0]], start=True, stop=True, is_transpose=True)

            def project(n, i, b, src, weight):
                turn_x(n, i, b, src)
                project_x(n, i, b, weight)

            def turn_x(n, i, b, src):
                pe.wait_ge(x_ready[n], NB if n == 0 else i + 1)
                for q in range(KB // 2):
                    k = b * KB + 2 * q
                    last = turned(hacc[:, b * BANK + q * P:b * BANK + (q + 1) * P], src[:, k:k + 2, :].rearrange("p k f -> p (k f)"))
                last.then_inc(xt_done[n], 1)

            def project_x(n, i, b, weight):
                pe.wait_ge(xT_ready[n], i + 1)
                for q in range(KB // 2):
                    last = mm(hacc[:, b * BANK + q * P:b * BANK + (q + 1) * P], xT[i % 2][:, q, :],
                              W2[:, weight, :], start=True, stop=True)
                last.then_inc(xw_done[n], 1)

            def first_product(s, p, k):
                h = k % 2
                return mm(tacc[h * F:(h + 1) * F, 0:PW], ez[:, k, :], nat[:, k, :],
                          start=(k < 2), stop=(k >= K - 2), skip_group_check=True)

            def second_product(s, which, n, first, last_panel=False):
                c, j = n // JP, n % JP
                for h in range(2):
                    last = mm(hacc[h * F:(h + 1) * F, c * BANK:(c + 1) * BANK], tv[which][:, j, :],
                              at[which][:, j, (2 * c + h) * BANK:(2 * c + h + 1) * BANK],
                              start=(first and j == 0), stop=(last_panel and j == JP - 1), skip_group_check=True)
                return last

            def buf(s, par_):
                return par_ if s == 0 else 1 - par_

            def back(s, p, par_):
                pe.wait_ge(tT_ready[s], p)
                for j in range(JP):
                    last = turned(turn[(par_ + BACK) % 2][:, j * P:(j + 1) * P], tT[:, j * P:(j + 1) * P])
                last.then_inc(back_done[s], 1)

            def slot(s, p, par_, q, first, transposes, second_first):
                idx = q + (q >= BACK)
                if q == BACK and not first:
                    if transposes:
                        pe.wait_ge(at_ready[s], p * NS + BACK - 2 + 1)
                    back(s, p, par_)
                if q % 2 == 0:
                    pe.wait_ge(nat_in[q // 2], 16 * (p + 1) if s == 0 else 16 * (p + NP))
                if transposes:
                    if idx == BACK + 2 and not first:
                        pe.wait_ge(back_read[s], p)
                    elif idx == BACK + 2:
                        pe.wait_ge(at_ready[s], BACK - 2 + 1)
                    elif not (first and q < 2):
                        prev = p * NS + (q - 2 if q < BACK or q > BACK + 1 else q - 1)
                        pe.wait_ge(at_ready[s], prev + 1)
                    bank = turn[(par_ + idx) % 2]
                    for kk in range(2):
                        for j in range(JP):
                            last = turned(bank[:, j * PW + kk * P:j * PW + (kk + 1) * P],
                                          nat[:, 2 * q + kk, j * P:(j + 1) * P])
                    last.then_inc(tr_done[s], 1)
                if first and q % (KB // 2) == 0:
                    pe.wait_ge(v_ready[s], q // (KB // 2) + 1)
                if q == 0 and not first:
                    pe.wait_ge(tT_ready[s], p)
                for kk in range(2):
                    last = first_product(s, p, 2 * q + kk)
                if q % 2 == 1:
                    last.then_inc(nat_used[s], 1)
                if q == P2_SLOT and not first:
                    pe.wait_ge(tv_ready[s], p)
                if q >= P2_SLOT and not first:
                    second_product(s, (buf(s, par_) + 1) % 2, q - P2_SLOT, second_first)

            def panel(s, p, par_, transposes=True, second_first=False):
                for q in range(NS):
                    slot(s, p, par_, q, False, transposes, second_first)

            def panels(s):
                panel(s, 1, 1, s == 0, True)
                if s == 1:
                    pe.sem_inc(tr_done[s], 2 * NS)
                with pe.Fori(1, NP // 2) as h:
                    panel(s, 2 * h, 0)
                    panel(s, 2 * h + 1, 1)
                pe.wait_ge(at_ready[s], NP * NS)
                back(s, NP, 0)
                pe.wait_ge(tv_ready[s], NP)
                banks = order(s)
                for i, c in enumerate(banks):
                    for j in range(JP):
                        last = second_product(s, buf(s, 1), c * JP + j, False, True)
                    last.then_inc(bank_done[s], 1)
                    if i in (1, 2):
                        turn_group(s, i - 1)

            def turn_group(s, i):
                c = order(s)[i]
                pe.wait_ge(hT_ready[s], i + 1)
                if i >= 2:
                    pe.wait_ge(*((sq_ready, max(2 * (i - 2), 1)) if s == 0 else (h_read, i - 1)))
                for q in range(4):
                    src = hT[:, c * BANK + q * P:c * BANK + (q + 1) * P]
                    dst = turn[i % 2][:, q * P:(q + 1) * P]
                    last = mm(dst, src, center[:, :], start=True, stop=True) if s == 0 else turned(dst, src)
                last.then_inc(h_back[s], 1)
                if s == 0:
                    for q in range(4):
                        last = mm(hacc[:, c * BANK + q * P:c * BANK + (q + 1) * P],
                                  hT[:, c * BANK + q * P:c * BANK + (q + 1) * P], centerg[:, :], start=True, stop=True)
                    last.then_inc(hg_back, 1)

            pe.wait_ge(in_small, 16 * 17)
            pe.wait_ge(consts, 12)
            turned(tacc[:, 0:K], dg[:, :]).then_inc(dg_done, 1)
            turn_x(0, 0, 0, xa)
            for b in range(NB):
                if b + 1 < NB:
                    turn_x(0, b + 1, b + 1, xa)
                project_x(0, b, b, 0 if b * KB < KU else 1)
            pe.wait_ge(centerg_ready, 1)
            for q in range(NS):
                slot(0, 0, 0, q, True, True, False)
            panels(0)
            for b in range(NB):
                if b + 2 < NB:
                    turn_group(0, b + 2)
                project(1, b, b, xb, 2)
                if b:
                    for q in range((b - 1) * KB // 2, b * KB // 2):
                        slot(1, 0, 0, q, True, False, False)
            for q in range((NB - 1) * KB // 2, NS):
                slot(1, 0, 0, q, True, False, False)
            panels(1)
            for i in range(NB):
                if i + 2 < NB:
                    turn_group(1, i + 2)
                project(2, i, order(1)[i], xb, 3)

            def weigh(r, n):
                for c in range(2):
                    pe.wait_ge(w_ready, (r * K + n) * 2 + c + 1)
                    last = mm(acc[c], s2[:, K - 1 - n, :], wr[c][n % 2][:, :], start=(n == 0), stop=(n == K - 1),
                              skip_group_check=True)
                last.then_inc(w_used, 1)

            def turn_out(r):
                for c in range(2):
                    pe.wait_ge(oT_ready[c], r + 1)
                    for q in range(4):
                        last = turned(turn[c][:, q * P:(q + 1) * P], hT[:, c * BANK + q * P:c * BANK + (q + 1) * P])
                    last.then_inc(o_back, 1)

            def row_group(r, first):
                for n in range(K):
                    j = K - 1 - n
                    if n % 8 == 0:
                        wait_alone(pe, mask_in[n // 8], r * 16 + 16)
                    for c in range(2):
                        cols = slice(c * BANK, (c + 1) * BANK)
                        if n > 0:
                            wait_alone(pe, bits_ready, (r * K + n - 1) * 2 + c + 1)
                            mm(cnt[c], rest[:, :], mask[:, j + 1, cols], start=False, stop=False,
                               skip_group_check=True)
                        mm(cnt[c], upto[:, :], mask[:, j, cols], start=(n == 0), stop=False,
                           skip_group_check=True).then_inc(cnt_done, 1)
                    if n == 1 and not first:
                        turn_out(r - 1)
                    if n == 1 and first:
                        pe.wait_ge(v_ready[2], NB)
                    if n > 0:
                        weigh(r, n - 1)
                weigh(r, K - 1)

            pe.wait_ge(v_ready[2], 2)
            row_group(0, True)
            with pe.Fori(1, NB) as r:
                row_group(r, False)
            turn_out(NB - 1)

        @block.scalar
        def _(act):
            copy = ACT.Copy

            def root(i, at_, n):
                act.wait_ge(var_ready, i + 1)
                nc.scalar.activation(sm[:, 3, at_:at_ + n], sm[:, 2, at_:at_ + n], ACT.Sqrt).then_inc(sd_ready, 1)

            def squares(i, semaphore, value, src, at_):
                act.wait_ge(semaphore, value)
                if i:
                    act.wait_ge(sq_ready, i)
                for k in range(KB):
                    last = nc.scalar.activation(junk[:, k, :],
                                                src[:, k, :] if len(src.shape) == 3 else src[:, k // 4, k % 4, :], ACT.Square,
                                                accum_out=sm[:, 1, at_ + k:at_ + k + 1])
                last.then_inc(sq_ready, 1)

            def project(n, i, b):
                act.wait_ge(xt_done[n], i + 1)
                if n == 0 and i >= 2:
                    act.wait_ge(xw_done[0], i - 1)
                nc.scalar.activation(xT[i % 2][:, :, :].rearrange("p q i -> p (q i)"),
                                     hacc[:, b * BANK:(b + 1) * BANK], copy).then_inc(xT_ready[n], 1)

            def panel(s, p, par_, first, reused):
                for q in range(NS):
                    idx = q + (q >= BACK)
                    if q == 0 and reused and s == 0:
                        act.wait_ge(mask_made, (p - 1) * NB)
                    act.wait_ge(tr_done[s], p * NS + q + 1)
                    nc.scalar.activation(at[par_ if s == 0 else 1 - par_][:, :, q * PW:(q + 1) * PW],
                                         turn[(par_ + idx) % 2][:, :].rearrange("p (j c) -> p j c", j=JP),
                                         copy).then_inc(at_ready[s], 1)
                    if q == SQRT_SLOT and s == 1 and not first:
                        root(NVARS0 + p - 1, 0, JP)

            def bank_out(s, i):
                c = order(s)[i]
                act.wait_ge(bank_done[s], i + 1)
                nc.scalar.activation(hT[:, c * BANK:(c + 1) * BANK], hacc[:, c * BANK:(c + 1) * BANK],
                                     copy).then_inc(hT_ready[s], 1)

            for b in range(NB):
                project(0, b, b)
            panel(0, 0, 0, True, False)
            panel(0, 1, 1, False, False)
            with act.Fori(1, NP // 2) as h:
                panel(0, 2 * h, 0, False, True)
                panel(0, 2 * h + 1, 1, False, True)
            root(0, 0, K)
            for m in range(NB):
                act.wait_ge(mask_out[m], 16 * NP)
            bank_out(0, 0)
            bank_out(0, 1)
            for t in range(NB + 2):
                if t + 2 < NB:
                    bank_out(0, t + 2)
                if t < NB:
                    squares(max(2 * t - 1, 0), h_back[0], t + 1,
                            turn[t % 2][:, :].rearrange("p (q h f) -> p h q f", q=4, h=2), t * KB)
                if t >= 2:
                    project(1, t - 2, t - 2)
                if 1 <= t <= NB:
                    squares(min(2 * t, 2 * NB - 1), cen_ready, t, hg[(t - 1) % 2], (t - 1) * KB)
                if t <= NB:
                    root(1 + t, max(t - 1, 0) * KB, (1 if t in (0, NB) else 2) * KB)

            act.wait_ge(mask_made, NP * NB)
            act.sem_inc(at_ready[1], 2 * NS)
            root(NVARS0, 0, JP)
            with act.Fori(1, NP // 2) as h:
                panel(1, 2 * h, 0, False, True)
                panel(1, 2 * h + 1, 1, False, True)
            root(NVARS0 + NP - 1, 0, JP)
            bank_out(1, 0)
            bank_out(1, 1)
            for t in range(NB + 1):
                if t + 2 < NB:
                    bank_out(1, t + 2)
                if t >= 1:
                    project(2, t - 1, order(1)[t - 1])
                if t < NB:
                    squares(2 * NB + t, cen_ready, NB + t + 1, hg[t % 2], order(1)[t] * KB)
                    root(NVARS0 + NP + t, order(1)[t] * KB, KB)

            def row_group(r, first):
                for n in range(K):
                    for c in range(2):
                        act.wait_ge(cnt_done, (r * K + n) * 2 + c + 1)
                        nc.scalar.activation(wbits[c][n % 2], cnt[c], ACT.Relu).then_inc(bits_ready, 1)
                    for c in range(2):
                        if n == FINISH + 16 * c + 2 * FROOT and not first:
                            root(NVARS0 + NVARS1 + 2 * (r - 1) + c, c * KB // 2, KB // 2)
                act.wait_ge(w_used, r * K + K)
                nc.scalar.activation(hT[:, 0:BANK], acc[0], copy).then_inc(oT_ready[0], 1)

            row_group(0, True)
            with act.Fori(1, NB) as r:
                row_group(r, False)
            for c in range(2):
                root(NVARS0 + NVARS1 + 2 * (NB - 1) + c, c * KB // 2, KB // 2)

        @block.vector
        def _(dve):
            V = nc.vector
            done = [0]

            def link(ins):
                done[0] = done[0] + 1
                ins.then_inc(chain, 1)
                dve.wait_ge(chain, done[0])

            def over_f(col, n):
                return col.rearrange("p (n a) -> p n a", a=1).broadcast_to([P, n, F])

            def over_n(row, n):
                return row.rearrange("p (a f) -> p a f", a=1).broadcast_to([P, n, F])

            def inverse_root(i, at_, n):
                v, sd, r0, u = (sm[:, c, at_:at_ + n] for c in (2, 3, 4, 5))
                dve.wait_ge(sd_ready, i + 1)
                link(V.reciprocal(r0, sd))
                link(V.scalar_tensor_tensor(u, r0, -0.5, r0, ALU.mult, ALU.mult))
                link(V.tensor_tensor(u, u, v, ALU.mult))
                link(V.scalar_tensor_tensor(u, u, 1.5, r0, ALU.add, ALU.mult))
                return u

            def less_mean(src, at_, n):
                mean = sm[:, 0, at_:at_ + n]
                link(V.tensor_reduce(mean, src, AX_X, ALU.add))
                link(V.tensor_scalar(mean, mean, 1.0 / F, None, ALU.mult))
                return V.tensor_tensor(src, src, over_f(mean, n), ALU.subtract)

            def variance(at_, n):
                V.tensor_scalar(sm[:, 2, at_:at_ + n], sm[:, 1, at_:at_ + n], 1.0 / F, LN_EPS,
                                ALU.mult, ALU.add).then_inc(var_ready, 1)

            dve.wait_ge(in_small, 16 * 17)
            dve.wait_ge(consts, 12)
            V.tensor_tensor(centerg[:, :].rearrange("p (n f) -> p n f", n=2), center[:, :].rearrange("p (n f) -> p n f", n=2),
                            over_n(rows[:, 0, :], 2), ALU.mult).then_inc(centerg_ready, 1)
            link(V.tensor_tensor(sm[:, 6, 0:1], par[:, 0:1], par[:, 1:2], ALU.mult))
            link(V.tensor_tensor(sm[:, 6, 1:2], par[:, 2:3], par[:, 3:4], ALU.mult))
            dve.wait_ge(dg_done, 1)
            link(V.tensor_scalar(g[:, 0:KU], tacc[:, 0:KU], sm[:, 6, 0:1], None, ALU.mult))
            V.tensor_scalar(g[:, KU:K], tacc[:, KU:K], sm[:, 6, 1:2], None, ALU.mult).then_inc(x_ready[0], NB)
            dve.wait_ge(x_ready[0], NB)

            def group(t, b):
                return t[:, b * KB:(b + 1) * KB, :]

            def bank(b):
                return hacc[:, b * BANK:(b + 1) * BANK].rearrange("p (n f) -> p n f", n=KB)

            for b in range(NB):
                dve.wait_ge(xw_done[0], b + 1)
                if b >= 2:
                    dve.wait_ge(v_ready[0], b - 1)
                link(V.tensor_tensor(hg[b % 2][:, :, :], bank(b), over_f(g[:, b * KB:(b + 1) * KB], KB), ALU.mult))
                V.tensor_tensor(group(ez, b), hg[b % 2][:, :, :], group(xa, b), ALU.add).then_inc(v_ready[0], 1)

            def take(s, p):
                dve.wait_ge(nat_used[s], (p + 1) * NG)
                return V.tensor_copy(tT[:, :], tacc[:, 0:PW]).then_inc(tT_ready[s], 1)

            def halves(par_):
                return turn[(par_ + BACK) % 2][:, 0:PW].rearrange("p (j h f) -> p j f h", j=JP, h=2)

            def masks(p, par_, m, first):
                rows_ = slice(m * RW, (m + 1) * RW)
                dve.wait_ge(at_ready[0], p * NS + MS * (m + 1))
                if not first:
                    dve.wait_ge(mask_out[m], p * 16)
                V.tensor_reduce(degp[:, bass.ds(p * JP, JP), m], at[par_][:, :, rows_], AX_X, ALU.add)
                V.tensor_scalar(mstage[m].rearrange("p (j r) -> p j r", j=JP), at[par_][:, :, rows_], 0.0, None,
                                ALU.not_equal, saturate=False).then_inc(mask_made, 1)

            def panel0(p, par_, first):
                if not first:
                    dve.wait_ge(back_done[0], p)
                    V.tensor_reduce(tv[1 - par_][:, :, :], halves(par_), AX_X, ALU.add).then_inc(tv_ready[0], 1)
                for m in range(NB - 1):
                    masks(p, par_, m, first)
                take(0, p)
                masks(p, par_, NB - 1, first)

            panel0(0, 0, True)
            panel0(1, 1, False)
            with dve.Fori(1, NP // 2) as h:
                panel0(2 * h, 0, False)
                panel0(2 * h + 1, 1, False)
            dve.wait_ge(back_done[0], NP)
            V.tensor_reduce(tv[1][:, :, :], halves(0), AX_X, ALU.add).then_inc(tv_ready[0], 1)

            dve.wait_ge(mask_made, NP * NB)
            link(V.tensor_reduce(sm[:, 0, :], degp[:, :, :], AX_X, ALU.add))
            link(V.tensor_scalar(sm[:, 0, :], sm[:, 0, :], 1.0, None, ALU.add))
            link(V.tensor_scalar(dinv[:, :], sm[:, 0, :], 0.0, None, ALU.is_gt))
            V.tensor_scalar(sm[:, 2, :], sm[:, 0, :], 2.0 ** -100, None, ALU.max).then_inc(var_ready, 1)
            u = inverse_root(0, 0, K)
            link(V.tensor_tensor(dinv[:, :], u, dinv[:, :], ALU.mult))

            def turned_group(s, i):
                dve.wait_ge(h_back[s], i + 1)
                return turn[i % 2][:, :].rearrange("p (q h f) -> p h q f", q=4, h=2)

            def by_half(t):
                return t.rearrange("p (h q) f -> p h q f", h=2)

            def first_norm_ends(b):
                w = hg[b % 2][:, :, :]
                u = sm[:, 5, b * KB:(b + 1) * KB]
                dve.wait_ge(hg_back, b + 1)
                if b >= 2:
                    dve.wait_ge(x_ready[1], b - 1)
                for h in range(2):
                    src = bank(b).rearrange("p (q h) f -> p h q f", h=2)[:, h, :, :]
                    ins = V.tensor_tensor(w[:, 4 * h:4 * h + 4, :], src, over_f(u[:, 4 * h:4 * h + 4], 4), ALU.mult)
                link(ins)
                link(V.tensor_tensor(w, w, group(xb, b), ALU.add))
                less_mean(w, b * KB, KB).then_inc(cen_ready, 1)

            def make_z(b):
                dve.wait_ge(xw_done[1], b + 1)
                V.tensor_tensor(group(ez, b), bank(b), over_f(dinv[:, b * KB:(b + 1) * KB], KB),
                                ALU.mult).then_inc(v_ready[1], 1)

            dve.wait_ge(u_ready, 2)
            for t in range(NB + 2):
                lo, n = max(t - 1, 0) * KB, (1 if t in (0, NB) else 2) * KB
                if 1 <= t <= NB:
                    first_norm_ends(t - 1)
                if t >= 2:
                    make_z(t - 2)
                if t <= NB:
                    dve.wait_ge(sq_ready, min(2 * t + 1, 2 * NB))
                    variance(lo, n)
                    inverse_root(1 + t, lo, n)
                if 1 <= t <= NB:
                    b = t - 1
                    V.tensor_tensor(group(xb, b), hg[b % 2][:, :, :], over_f(sm[:, 5, b * KB:(b + 1) * KB], KB),
                                    ALU.mult).then_inc(x_ready[1], 1)

            def x2_of(p, par_, column_block):
                y, sq = cy, cc
                dve.wait_ge(back_done[1], p)
                blk = bass.ds(column_block, JP)
                V.tensor_reduce(y, halves(par_), AX_X, ALU.add).then_inc(back_read[1], 1)
                dve.wait_ge(back_read[1], p)
                link(V.tensor_tensor(y, y, ez[:, blk, :], ALU.add))
                link(V.tensor_tensor(y, y, over_f(dinv[:, blk], JP), ALU.mult))
                link(V.tensor_tensor(y, y, over_n(rows[:, 2, :], JP), ALU.add))
                link(V.scalar_tensor_tensor(y, y, 0.0, xb[:, blk, :], ALU.max, ALU.add))
                link(less_mean(y, 0, JP))
                link(V.tensor_tensor(sq, y, y, ALU.mult))
                link(V.tensor_reduce(sm[:, 1, 0:JP], sq, AX_X, ALU.add))
                variance(0, JP)
                u = inverse_root(NVARS0 + p - 1, 0, JP)
                dst = tv[par_][:, :, :]
                V.tensor_tensor(dst, y, over_f(u, JP), ALU.mult).then_inc(tv_ready[1], 1)
                dve.wait_ge(tv_ready[1], p)
                V.tensor_copy(xa[:, blk, :], dst)
                link(V.tensor_scalar(sq, dst, -B_CONST, F_CONST, ALU.mult, ALU.add))
                link(V.tensor_tensor(xb[:, blk, :], sq, dst, ALU.add))

            X2_LINKS = 4 + 3 + 2 + 4 + 2

            take(1, 0)
            x2_of(1, 1, (NP - 1) * JP)
            take(1, 1)
            x2_of(2, 0, (NP - 2) * JP)
            take(1, 2)
            before = done[0]
            with dve.Fori(1, NP // 2 - 1) as h:
                done[0] = before + (2 * h - 2) * X2_LINKS
                x2_of(2 * h + 1, 1, (2 * h - 2) * JP)
                take(1, 2 * h + 1)
                x2_of(2 * h + 2, 0, (2 * h - 1) * JP)
                take(1, 2 * h + 2)
            done[0] = before + (NP - 4) * X2_LINKS
            x2_of(NP - 1, 1, (NP - 4) * JP)
            take(1, NP - 1)
            x2_of(NP, 0, (NP - 3) * JP)

            def x3_starts(i):
                b = order(1)[i]
                w = hg[i % 2][:, :, :]
                outer = sm[:, 6, b * KB:(b + 1) * KB]
                src = turned_group(1, i)
                if i >= 2:
                    dve.wait_ge(x_ready[2], i - 1)
                V.tensor_tensor(by_half(w), src, by_half(group(xa, b)), ALU.mult).then_inc(h_read, 1)
                dve.wait_ge(h_read, i + 1)
                link(V.tensor_reduce(outer, w, AX_X, ALU.add))
                link(V.tensor_scalar(outer, outer, R_CONST, None, ALU.mult))
                link(V.tensor_tensor(w, group(xb, b), over_f(outer, KB), ALU.subtract))
                less_mean(w, b * KB, KB).then_inc(cen_ready, 1)

            def x3_ends(i):
                b = order(1)[i]
                u = inverse_root(NVARS0 + NP + i, b * KB, KB)
                V.tensor_tensor(group(xb, b), hg[i % 2][:, :, :], over_f(u, KB), ALU.mult).then_inc(x_ready[2], 1)

            def make_s(i):
                b = order(1)[i]
                dve.wait_ge(xw_done[2], i + 1)
                high, low = group(s2, b)[:, :, 0:F], group(s2, b)[:, :, F:2 * F]
                link(V.tensor_scalar(high, bank(b), W_UNIT, None, ALU.mult))
                V.scalar_tensor_tensor(low, bank(b), W_UNIT, high.bitcast(F32), ALU.mult, ALU.subtract).then_inc(v_ready[2], 1)

            for t in range(NB + 1):
                if t >= 1:
                    x3_ends(t - 1)
                if t < NB:
                    x3_starts(t)
                if t >= 1:
                    make_s(t - 1)
                if t < NB:
                    dve.wait_ge(sq_ready, 2 * NB + t + 1)
                    variance(order(1)[t] * KB, KB)

            HK = KB // 2

            def finish(r, c, i):
                blk = bass.ds(r * KB + c * HK, HK)
                o, sq = hg[0][:, c * HK:(c + 1) * HK, :], hg[1][:, c * HK:(c + 1) * HK, :]
                mean, ss = sm[:, 0, c * HK:(c + 1) * HK], sm[:, 1, c * HK:(c + 1) * HK]
                if i == 0:
                    dve.wait_ge(o_back, r * 2 + c + 1)
                    link(V.tensor_reduce(o, turn[c][:, :].rearrange("p (q h f) -> p q f h", q=4, h=2), AX_X, ALU.add))
                elif i == 1:
                    link(V.tensor_tensor(o, o, xb[:, blk, :], ALU.add))
                elif i == 2:
                    link(V.tensor_reduce(mean, o, AX_X, ALU.add))
                    link(V.tensor_scalar(mean, mean, 1.0 / F, None, ALU.mult))
                elif i == 3:
                    link(V.tensor_tensor(o, o, over_f(mean, HK), ALU.subtract))
                elif i == 4:
                    link(V.tensor_tensor(sq, o, o, ALU.mult))
                elif i == FROOT:
                    link(V.tensor_reduce(ss, sq, AX_X, ALU.add))
                    variance(c * HK, HK)
                elif i == 6:
                    inverse_root(NVARS0 + NVARS1 + r * 2 + c, c * HK, HK)
                elif i == 7:
                    V.tensor_tensor(xa[:, blk, :], o, over_f(sm[:, 5, c * HK:(c + 1) * HK], HK),
                                    ALU.mult).then_inc(y_ready, 1)
                    dve.wait_ge(y_ready, r * 2 + c + 1)

            FINISH_LINKS = 2 * (1 + 1 + 2 + 1 + 1 + 1 + 4)

            def row_group(r, first):
                for n in range(K):
                    for c in range(2):
                        dve.wait_ge(bits_ready, (r * K + n) * 2 + c + 1)
                        V.tensor_copy(wr[c][n % 2][:, :], wbits[c][n % 2].bitcast(BF16)).then_inc(w_ready, 1)
                    for c in range(2):
                        i, odd = divmod(n - FINISH - 16 * c, 2)
                        if not first and not odd and 0 <= i < FSTEPS:
                            finish(r - 1, c, i)
                dve.wait_ge(w_used, r * K + K)
                V.tensor_copy(hT[:, BANK:2 * BANK], acc[1]).then_inc(oT_ready[1], 1)

            row_group(0, True)
            dve.wait_ge(xb3_ready, 1)
            before = done[0]
            with dve.Fori(1, NB) as r:
                done[0] = before + (r - 1) * FINISH_LINKS
                row_group(r, False)
            done[0] = before + (NB - 1) * FINISH_LINKS
            for i in range(FSTEPS):
                for c in range(2):
                    finish(NB - 1, c, i)


_INS = ['x', 'adj', 'L0_gnn_W_u', 'L0_gnn_diag_u', 'L0_gnn_par_u', 'L0_gnn_W_i', 'L0_gnn_diag_i', 'L0_gnn_par_i',
        'L0_gnn_ln_gamma', 'L0_gnn_ln_beta', 'L1_gnn_W', 'L1_gnn_b', 'L3_gnn_weight', 'L3_gnn_bias']


def kernel(**inputs):
    import numpy as _np
    import concourse.bacc as _bacc
    from concourse import mybir as _mybir
    from concourse.bass_utils import run_bass_kernel_spmd as _run

    nc = _bacc.Bacc("TRN2", target_bir_lowering=False, num_devices=1)
    arrays, args = {}, []
    for name in _INS:
        a = _np.ascontiguousarray(inputs[name])
        arrays[f"in_{name}"] = a
        args.append(nc.dram_tensor(f"in_{name}", a.shape, _mybir.dt.from_np(a.dtype), kind="ExternalInput").ap())
    shape = inputs['x'].shape
    args.append(nc.dram_tensor("out_x", shape, F32, kind="ExternalOutput").ap())
    resnorm_kernel(nc, *args)
    r = _run(nc, [arrays], core_ids=[0])
    return r.results[0]["out_x"]
```

```python
from contextlib import ExitStack

import concourse.bass as bass
from concourse import mybir

P = 128
F32 = mybir.dt.float32
F32R = mybir.dt.float32r
BF16 = mybir.dt.bfloat16
I16 = mybir.dt.int16
FP8 = mybir.dt.float8e4
U8 = mybir.dt.uint8
ALU = mybir.AluOpType
ACT = mybir.ActivationFunctionType
AX_X = mybir.AxisListType.X
BANK = 512

LN_EPS = 1e-5
F_CONST, B_CONST, R_CONST = 1.0, 0.1, 0.01
MAX_NEIGH = 100
STEP = 128.0
W_UNIT = 2.0 ** (127 - MAX_NEIGH)


def resnorm_kernel(nc, x, adj, W_u, diag_u, par_u, W_i, diag_i, par_i, gamma, beta, W1, b1, W3, b3, out):
    N, F = x.shape
    K = N // P
    JP = 2
    PW = JP * P
    NP = N // PW
    KU = diag_u.shape[0] // P
    GK = 4
    NG = K // GK
    NS = K // 2
    BACK = 4
    SQRT_SLOT = 8
    NB = 5
    KB = K // NB
    RW = KB * P
    MS = RW // PW
    assert N == NB * 2 * BANK and NS == 2 * NB * JP and NP % 2 == 0 and NP >= 4 and 2 * F == P

    x_d = x.rearrange("(k p) f -> p k f", p=P)
    out_d = out.rearrange("(k p) f -> p k f", p=P)
    adj_d = adj.rearrange("(k p) c -> p k c", p=P)
    mask_d = nc.dram_tensor("mask_t", [NP, NB, P, JP * RW], U8, kind="Internal").ap()

    ctx = ExitStack()
    with ctx:
        def sb(name, shape, dt=F32):
            return ctx.enter_context(nc.sbuf_tensor(name, shape, dt))

        def sem(name):
            return ctx.enter_context(nc.semaphore(name))

        xa = sb("xa", [P, K, F])
        xb = sb("xb", [P, K, F])
        ez = sb("ez", [P, K, F])
        at = [sb(f"at{i}", [P, JP, N]) for i in range(2)]
        nat = sb("nat", [P, K, PW])
        mask = nat[:, :, :].rearrange("p k c -> p (k c)").bitcast(FP8).rearrange("p (j r) -> p j r", j=K)
        hT = sb("hT", [P, NB * BANK])
        mstage = [hT[:, m * BANK:(m + 1) * BANK].bitcast(FP8) for m in range(NB)]
        xT = [sb(f"xT{i}", [P, KB // 2, P]) for i in range(2)]
        hg = [sb(f"hg{i}", [P, KB, F]) for i in range(2)]
        junk = sb("junk", [P, KB, F])
        x2_work, x2_work2 = junk[:, 0:JP, :], junk[:, JP:2 * JP, :]
        tT = sb("tT", [P, PW])
        tv = [sb(f"tv{i}", [P, JP, F]) for i in range(2)]
        s2 = sb("s2", [P, K, 2 * F], F32R)
        wr = [[sb(f"wr{c}{i}", [P, BANK], F32R) for i in range(2)] for c in range(2)]
        wbits = [[at[0][:, 0, (2 * c + i) * BANK:(2 * c + i) * BANK + BANK // 2].bitcast(I16) for i in range(2)]
                 for c in range(2)]
        W2 = sb("W2", [P, 4, P])
        ident = sb("ident", [P, P])
        center = sb("center", [P, P])
        centerg = sb("centerg", [P, P])
        upto = sb("upto", [P, P], BF16)
        rest = sb("rest", [P, P], BF16)
        rows = sb("rows", [P, 4, F])
        par = sb("par", [P, 4])
        dg = sb("dg", [K, P])
        g = sb("g", [P, K])
        degp = sb("degp", [P, K, NB])
        dinv = sb("dinv", [P, K])
        sm = sb("sm", [P, 7, K])

        hacc = ctx.enter_context(nc.psum_tensor("hacc", [P, NB * BANK], F32))
        tacc = ctx.enter_context(nc.psum_tensor("tacc", [P, BANK], F32))
        turn = [ctx.enter_context(nc.psum_tensor(f"turn{i}", [P, BANK], F32)) for i in range(2)]

        in_factors = sem("in_factors")
        in_Wu, in_Wi = sem("in_Wu"), sem("in_Wi")
        in_x = [sem(f"in_x{b}") for b in range(NB)]
        in_late = sem("in_late")
        made_zero = sem("made_zero")
        consts = sem("consts")
        nat_in = [sem(f"nat_in{i}") for i in range(NG)]
        mask_in = [sem(f"mask_in{i}") for i in range(NB)]
        mask_out = [sem(f"mask_out{i}") for i in range(NB)]
        out_done = sem("out_done")
        nat_used = [sem(f"nat_used{s}") for s in range(2)]
        tr_done = [sem(f"tr_done{s}") for s in range(2)]
        at_ready = [sem(f"at_ready{s}") for s in range(2)]
        tT_ready = [sem(f"tT_ready{s}") for s in range(2)]
        back_done = [sem(f"back_done{s}") for s in range(2)]
        tv_ready = [sem(f"tv_ready{s}") for s in range(2)]
        back_read = [tv_ready[0], sem("back_read1")]
        mask_made = sem("mask_made")
        u_ready = sem("u_ready")
        xb3_ready = sem("xb3_ready")
        cen_ready = sem("cen_ready")
        sq_ready = sem("sq_ready")
        bank_done = [sem(f"bank_done{s}") for s in range(2)]
        var_ready = sem("var_ready")
        sd_ready = sem("sd_ready")
        chain = sem("chain")
        hT_ready = [sem(f"hT_ready{s}") for s in range(2)]
        h_back = [sem(f"h_back{s}") for s in range(2)]
        h_read = sem("h_read")
        outer_ready = sem("outer_ready")
        less_outer = sem("less_outer")
        sq3_ready = sem("sq3_ready")
        high_ready = sem("high_ready")
        hg_back = sem("hg_back")
        centerg_ready = sem("centerg_ready")
        x_ready = [None] + [sem(f"x_ready{s}") for s in (1, 2)]
        xt_done = [sem(f"xt_done{s}") for s in range(3)]
        xT_ready = [sem(f"xT_ready{s}") for s in range(3)]
        xw_done = [sem(f"xw_done{s}") for s in range(3)]
        v_ready = [sem(f"v_ready{s}") for s in range(3)]
        dg_done = sem("dg_done")
        cnt_done = sem("cnt_done")
        bits_ready = sem("bits_ready")
        w_ready = sem("w_ready")
        w_used = sem("w_used")
        oT_ready = [sem(f"oT_ready{c}") for c in range(2)]
        o_back = sem("o_back")
        y_ready = sem("y_ready")

        passed = {nc.sync: sem("passed_sp"), nc.tensor: sem("passed_pe")}

        NVARS0, NVARS1 = 1 + NB + 1, NP + NB

        cnt = [hacc[:, b * BANK:(b + 1) * BANK] for b in (4, 3)]
        acc = [hacc[:, b * BANK:(b + 1) * BANK] for b in (2, 1)]
        FINISH, FSTEPS, FROOT = 4, 8, 5

        LEAD = 2 * KB
        (T_TURN, T_PRODUCT, T_OUTER, T_MEAN, T_CENTER, T_VAR, T_ROOT, T_INVERSE, T_END, T_XT, T_XT_OUT,
         T_XW, T_HIGH, T_LOW) = -1, 0, 1, 3, 4, 6, 7, 8, 10, 11, 12, 13, 14, 15

        def due(n, d):
            i, off = divmod(n + LEAD - d, KB)
            return [i] if off == 0 and 0 <= i < NB else []

        def bank_of(b):
            return hacc[:, b * BANK:(b + 1) * BANK]

        pw3 = [tacc, bank_of(0)]

        def order(s):
            return list(range(NB)) if s == 0 else list(range(NB - 1, -1, -1))

        block = ctx.enter_context(nc.Block())

        def wait_alone(eng, semaphore, value):
            eng.wait_ge(semaphore, value)
            eng.sem_inc(passed[eng], 1)

        @block.sync
        def _(sp):
            def load_x(b):
                sp.dma_start(xa[:, b * KB:(b + 1) * KB, :], x_d[:, b * KB:(b + 1) * KB, :]).then_inc(in_x[b], 16)

            def load_weight(i, w, semaphore):
                for h in range(2):
                    sp.dma_start(W2[h * F:(h + 1) * F, i, h * F:(h + 1) * F], w).then_inc(semaphore, 16)

            load_x(0)
            sp.wait_ge(made_zero, 1)
            load_weight(0, W_u, in_Wu)
            load_x(1)
            sp.dma_start(dg[0:KU, :], diag_u.rearrange("(k p) -> k p", p=P)).then_inc(in_factors, 16)
            sp.dma_start(dg[KU:K, :], diag_i.rearrange("(k p) -> k p", p=P)).then_inc(in_factors, 16)
            for i, v in enumerate((par_u, par_i)):
                sp.dma_start(par[:, 2 * i:2 * i + 2], v.rearrange("(a n) -> a n", a=1).broadcast_to([P, 2])).then_inc(in_factors, 16)
            load_x(2)
            load_weight(1, W_i, in_Wi)
            for b in range(3, NB):
                load_x(b)

            def load(column, grp):
                sp.dma_start(nat[:, GK * grp:GK * (grp + 1), :],
                             adj_d[:, GK * grp:GK * (grp + 1), bass.ds(column, PW)]).then_inc(nat_in[grp], 16)

            def store_mask(p, m):
                sp.dma_start(mask_d[bass.ds(p, 1), m, :, :].rearrange("a p c -> p (a c)"),
                             mstage[m].bitcast(U8)).then_inc(mask_out[m], 16)

            def load_group(s, p, grp, column):
                sp.wait_ge(nat_used[s], p * NG + grp + 1)
                load(column, grp)

            for grp in range(NG):
                load(0, grp)
            for i, v in enumerate((gamma, beta, b1, b3)):
                sp.dma_start(rows[:, i, :], v.rearrange("(a n) -> a n", a=1).broadcast_to([P, F])).then_inc(in_late, 16)
            for i, w in enumerate((W1, W3)):
                load_weight(2 + i, w, in_late)
            with sp.Fori(0, NP - 1) as p:
                for m in range(NB):
                    wait_alone(sp, mask_made, p * NB + m + 1)
                    store_mask(p, m)
                    for grp in (2 * m, 2 * m + 1):
                        load_group(0, p, grp, (p + 1) * PW)
            for m in range(NB):
                sp.wait_ge(mask_made, (NP - 1) * NB + m + 1)
                store_mask(NP - 1, m)

            for grp in range(NG):
                load_group(1, 0, grp, (NP - 2) * PW)
            with sp.Fori(1, NP - 1) as p:
                for grp in range(NG):
                    load_group(1, p, grp, (p - 1) * PW)

            def load_mask(r, q):
                lo = NP - 4 * (q + 1)
                sp.dma_start(mask.bitcast(U8)[:, 2 * lo:2 * lo + 8, :].rearrange("p (n j) r -> p n (j r)", j=JP),
                             mask_d[lo:lo + 4, bass.ds(r, 1), :, :].rearrange("n a p c -> p (n a) c")).then_inc(mask_in[q], 16)

            sp.wait_ge(nat_used[1], NP * NG)
            for m in range(NB):
                sp.wait_ge(mask_out[m], 16 * NP)
            for q in range(NB):
                load_mask(0, q)
            with sp.Fori(1, NB) as r:
                for q in range(NB):
                    wait_alone(sp, w_used, (r - 1) * K + 8 * (q + 1))
                    load_mask(r, q)
            with sp.Fori(0, NB) as r:
                wait_alone(sp, y_ready, 2 * r + 2)
                sp.dma_start(out_d[:, bass.ds(r * KB, KB), :], xa[:, bass.ds(r * KB, KB), :]).then_inc(out_done, 16)
            sp.wait_ge(out_done, 16 * NB)

        @block.gpsimd
        def _(pool):
            pool.memset(W2[:, :, :], 0.0).then_inc(made_zero, 1)
            pool.memset(ident[:, :], 0.0).then_inc(consts, 1)
            pool.memset(center[:, :], -1.0 / F).then_inc(consts, 1)
            pool.memset(upto[:, :], -STEP).then_inc(consts, 1)
            pool.memset(rest[:, :], -STEP).then_inc(consts, 1)
            pool.wait_ge(consts, 4)
            pool.affine_select(out=ident[:, :], in_=ident[:, :], compare_op=ALU.not_equal, fill=1.0,
                               base=0, pattern=[[-1, P]], channel_multiplier=1).then_inc(consts, 1)
            pool.affine_select(out=upto[:, :], in_=upto[:, :], compare_op=ALU.is_ge, fill=0.0,
                               base=0, pattern=[[-1, P]], channel_multiplier=1).then_inc(consts, 1)
            pool.affine_select(out=rest[:, :], in_=rest[:, :], compare_op=ALU.is_ge, fill=0.0,
                               base=0, pattern=[[1, P]], channel_multiplier=-1).then_inc(consts, 1)
            pool.wait_ge(consts, 7)
            pool.memset(center[0:F, F:P], 0.0).then_inc(consts, 1)
            pool.memset(center[F:P, 0:F], 0.0).then_inc(consts, 1)
            pool.wait_ge(consts, 9)
            pool.affine_select(out=center[:, :], in_=center[:, :], compare_op=ALU.not_equal, fill=1.0 - 1.0 / F,
                               base=0, pattern=[[-1, P]], channel_multiplier=1).then_inc(consts, 1)
            pool.affine_select(out=upto[:, :], in_=upto[:, :], compare_op=ALU.not_equal, fill=STEP * MAX_NEIGH,
                               base=0, pattern=[[-1, P]], channel_multiplier=1).then_inc(consts, 1)
            pool.affine_select(out=rest[:, :], in_=rest[:, :], compare_op=ALU.not_equal,
                               fill=-STEP * (MAX_NEIGH + 1),
                               base=0, pattern=[[-1, P]], channel_multiplier=1).then_inc(consts, 1)
            pool.wait_ge(v_ready[0], NB)
            pool.wait_ge(in_late, 16 * 8)
            pool.tensor_scalar(xb[:, :, :], xa[:, :, :], 2.0, None, ALU.mult).then_inc(u_ready, 1)
            pool.wait_ge(u_ready, 1)
            pool.tensor_tensor(xb[:, :, :], xb[:, :, :],
                               rows[:, 1, :].rearrange("p (a f) -> p a f", a=1).broadcast_to([P, K, F]),
                               ALU.add).then_inc(u_ready, 1)
            for n in range(-LEAD, K):
                for i in due(n, T_OUTER):
                    b, w = order(1)[i], hg[i % 2][:, :, :]
                    pool.wait_ge(outer_ready, i + 1)
                    outer = sm[:, 6, b * KB:(b + 1) * KB].rearrange("p (n a) -> p n a", a=1).broadcast_to([P, KB, F])
                    pool.tensor_tensor(w, xb[:, b * KB:(b + 1) * KB, :], outer, ALU.subtract).then_inc(less_outer, 1)
                for i in due(n, T_CENTER):
                    w = hg[i % 2][:, :, :]
                    pool.wait_ge(cen_ready, NB + i + 1)
                    if i:
                        pool.wait_ge(var_ready, NVARS0 + NP + i)
                    pool.tensor_tensor(junk[:, :, :], w, w, ALU.mult).then_inc(sq3_ready, 1)
            pool.wait_ge(xt_done[2], NB)
            pool.tensor_tensor(xb[:, :, :], xb[:, :, :],
                               rows[:, 3, :].rearrange("p (a f) -> p a f", a=1).broadcast_to([P, K, F]),
                               ALU.add).then_inc(xb3_ready, 1)

        @block.tensor
        def _(pe):
            mm = nc.tensor.matmul

            def turned(dst, src):
                return mm(dst, src, ident[0:src.shape[0], 0:src.shape[0]], start=True, stop=True, is_transpose=True)

            def turn_x(n, i, b, src, dst):
                pe.wait_ge(*((in_x[b], 16) if n == 0 else (x_ready[n], i + 1)))
                for q in range(KB // 2):
                    k = b * KB + 2 * q
                    last = turned(dst[:, q * P:(q + 1) * P], src[:, k:k + 2, :].rearrange("p k f -> p (k f)"))
                last.then_inc(xt_done[n], 1)

            def project_x(n, i, dst, weight):
                pe.wait_ge(xT_ready[n], i + 1)
                for q in range(KB // 2):
                    last = mm(dst[:, q * P:(q + 1) * P], xT[i % 2][:, q, :],
                              W2[:, weight, :], start=True, stop=True)
                last.then_inc(xw_done[n], 1)

            def first_product(s, p, k):
                h = k % 2
                return mm(tacc[h * F:(h + 1) * F, 0:PW], ez[:, k, :], nat[:, k, :],
                          start=(k < 2), stop=(k >= K - 2), skip_group_check=True)

            def second_product(s, which, n, first, last_panel=False):
                c, j = n // JP, n % JP
                for h in range(2):
                    last = mm(hacc[h * F:(h + 1) * F, c * BANK:(c + 1) * BANK], tv[which][:, j, :],
                              at[which][:, j, (2 * c + h) * BANK:(2 * c + h + 1) * BANK],
                              start=(first and j == 0), stop=(last_panel and j == JP - 1), skip_group_check=True)
                return last

            def buf(s, par_):
                return par_ if s == 0 else 1 - par_

            def back(s, p, par_):
                pe.wait_ge(tT_ready[s], p)
                for j in range(JP):
                    last = turned(turn[(par_ + BACK) % 2][:, j * P:(j + 1) * P], tT[:, j * P:(j + 1) * P])
                last.then_inc(back_done[s], 1)


            def load_is_there(s, p, q):
                pe.wait_ge(nat_in[q // 2], 16 * (p + 1) if s == 0 else 16 * (p + NP))

            def transpose_slot(s, p, par_, q, first):
                idx = q + (q >= BACK)
                if idx == BACK + 2 and not first:
                    pe.wait_ge(back_read[s], p)
                elif idx == BACK + 2:
                    pe.wait_ge(at_ready[s], BACK - 2 + 1)
                elif not (first and q < 2):
                    prev = p * NS + (q - 2 if q < BACK or q > BACK + 1 else q - 1)
                    pe.wait_ge(at_ready[s], prev + 1)
                bank = turn[(par_ + idx) % 2]
                for kk in range(2):
                    for j in range(JP):
                        last = turned(bank[:, j * PW + kk * P:j * PW + (kk + 1) * P],
                                      nat[:, 2 * q + kk, j * P:(j + 1) * P])
                last.then_inc(tr_done[s], 1)

            def first_slot(s, p, q, first):
                if first and q % (KB // 2) == 0:
                    pe.wait_ge(v_ready[s], q // (KB // 2) + 1)
                if q == 0 and not first:
                    pe.wait_ge(tT_ready[s], p)
                for kk in range(2):
                    last = first_product(s, p, 2 * q + kk)
                if q % 2 == 1:
                    last.then_inc(nat_used[s], 1)

            def second_slot(s, p, par_, q, each, second_first):
                start = NS - NB * JP // each
                if q == start:
                    pe.wait_ge(tv_ready[s], p)
                if q >= start:
                    for n in range(each * (q - start), each * (q - start + 1)):
                        second_product(s, (buf(s, par_) + 1) % 2, n, second_first)

            def two_slots(s, p, par_, q, first, transposes, second_first, second=True):
                turning = q == BACK and not first
                load_is_there(s, p, q)
                if turning:
                    if transposes:
                        pe.wait_ge(at_ready[s], p * NS + BACK - 2 + 1)
                    back(s, p, par_)
                if transposes:
                    transpose_slot(s, p, par_, q, first)
                if transposes and not turning:
                    transpose_slot(s, p, par_, q + 1, first)
                first_slot(s, p, q, first)
                if transposes and turning:
                    transpose_slot(s, p, par_, q + 1, first)
                first_slot(s, p, q + 1, first)
                if second and not first:
                    for i in (q, q + 1):
                        second_slot(s, p, par_, i, 1 if transposes else 2, second_first)

            def panel(s, p, par_, transposes=True, second_first=False, second=True):
                for q in range(0, NS, 2):
                    two_slots(s, p, par_, q, False, transposes, second_first, second)

            def panels(s):
                panel(s, 1, 1, s == 0, True)
                if s == 1:
                    pe.sem_inc(tr_done[s], 2 * NS)
                with pe.Fori(1, NP // 2 - 1) as h:
                    panel(s, 2 * h, 0)
                    panel(s, 2 * h + 1, 1)
                panel(s, NP - 2, 0)
                panel(s, NP - 1, 1, second=False)
                pe.wait_ge(at_ready[s], NP * NS)
                back(s, NP, 0)
                banks, early = order(s), (2, 3)[s]

                def bank_adds(p, c, last_panel):
                    for j in range(JP):
                        last = second_product(s, buf(s, p % 2), c * JP + j, False, last_panel)
                    return last

                pe.wait_ge(tv_ready[s], NP - 1)
                for c in banks[:early]:
                    bank_adds(NP - 2, c, False)
                pe.wait_ge(tv_ready[s], NP)
                for i, c in enumerate(banks):
                    if i >= early:
                        bank_adds(NP - 2, c, False)
                    bank_adds(NP - 1, c, True).then_inc(bank_done[s], 1)
                    if i in (1, 2):
                        turn_group(s, i - 1)

            def turn_group(s, i):
                c = order(s)[i]
                if s == 0 and i == 0:
                    pe.wait_ge(centerg_ready, 1)
                pe.wait_ge(hT_ready[s], i + 1)
                if i >= 2:
                    pe.wait_ge(*((sq_ready, max(2 * (i - 2), 1)) if s == 0 else (h_read, i - 1)))
                for q in range(4):
                    src = hT[:, c * BANK + q * P:c * BANK + (q + 1) * P]
                    dst = turn[i % 2][:, q * P:(q + 1) * P]
                    last = mm(dst, src, center[:, :], start=True, stop=True) if s == 0 else turned(dst, src)
                last.then_inc(h_back[s], 1)
                if s == 0:
                    for q in range(4):
                        last = mm(hacc[:, c * BANK + q * P:c * BANK + (q + 1) * P],
                                  hT[:, c * BANK + q * P:c * BANK + (q + 1) * P], centerg[:, :], start=True, stop=True)
                    last.then_inc(hg_back, 1)

            pe.wait_ge(consts, 12)
            turn_x(0, 0, 0, xa, bank_of(0))
            for b in range(NB):
                if b + 1 < NB:
                    turn_x(0, b + 1, b + 1, xa, bank_of(b + 1))
                users = b * KB < KU
                pe.wait_ge(in_Wu if users else in_Wi, 16 * 2)
                project_x(0, b, bank_of(b), 0 if users else 1)
                if b == 0:
                    pe.wait_ge(in_factors, 16 * 4)
                    turned(tacc[:, 0:K], dg[:, :]).then_inc(dg_done, 1)
            for q in range(0, NS, 2):
                two_slots(0, 0, 0, q, True, True, False)
            panels(0)
            for b in range(NB):
                if b + 2 < NB:
                    turn_group(0, b + 2)
                ready = [(b - 1) * KB // 2 + q for q in range(KB // 2)] if b else []
                for q in ready[:2]:
                    first_slot(1, 0, q, True)
                turn_x(1, b, b, xb, bank_of(b))
                for q in ready[2:]:
                    first_slot(1, 0, q, True)
                pe.wait_ge(in_late, 16 * 8)
                project_x(1, b, bank_of(b), 2)
            for q in range((NB - 1) * KB // 2, NS):
                first_slot(1, 0, q, True)
            panels(1)

            def weigh(r, n):
                for c in range(2):
                    pe.wait_ge(w_ready, (r * K + n) * 2 + c + 1)
                    last = mm(acc[c], s2[:, K - 1 - n, :], wr[c][n % 2][:, :], start=(n == 0), stop=(n == K - 1),
                              skip_group_check=True)
                last.then_inc(w_used, 1)

            def turn_out(r):
                for c in range(2):
                    pe.wait_ge(oT_ready[c], r + 1)
                    for q in range(4):
                        last = turned(turn[c][:, q * P:(q + 1) * P], hT[:, c * BANK + q * P:c * BANK + (q + 1) * P])
                    last.then_inc(o_back, 1)

            def groups_step(n):
                for i in due(n, T_TURN):
                    if i >= 2:
                        turn_group(1, i)
                for i in due(n, T_XT):
                    if i == 0:
                        pe.wait_ge(hT_ready[1], NB)
                    if i >= 2:
                        pe.wait_ge(v_ready[2], i - 1)
                    turn_x(2, i, order(1)[i], xb, pw3[i % 2])
                for i in due(n, T_XW):
                    project_x(2, i, pw3[i % 2], 3)

            def row_group(r, first):
                for n in range(K):
                    j = K - 1 - n
                    if n % 8 == 0:
                        wait_alone(pe, mask_in[n // 8], r * 16 + 16)
                    for c in range(2):
                        cols = slice(c * BANK, (c + 1) * BANK)
                        if n > 0 or not first:
                            wait_alone(pe, bits_ready, (r * K + n - 1) * 2 + c + 1)
                        if n > 0:
                            mm(cnt[c], rest[:, :], mask[:, j + 1, cols], start=False, stop=False,
                               skip_group_check=True)
                        mm(cnt[c], upto[:, :], mask[:, j, cols], start=(n == 0), stop=False,
                           skip_group_check=True).then_inc(cnt_done, 1)
                    if n == 1 and not first:
                        turn_out(r - 1)
                    if n % KB == 1 and first:
                        pe.wait_ge(v_ready[2], n // KB + 1)
                    if n > 0:
                        weigh(r, n - 1)
                    elif not first:
                        weigh(r - 1, K - 1)
                    if first:
                        groups_step(n)

            for n in range(-LEAD, 0):
                groups_step(n)
            row_group(0, True)
            with pe.Fori(1, NB) as r:
                row_group(r, False)
            weigh(NB - 1, K - 1)
            turn_out(NB - 1)

        @block.scalar
        def _(act):
            copy = ACT.Copy

            def root(i, at_, n):
                act.wait_ge(var_ready, i + 1)
                nc.scalar.activation(sm[:, 3, at_:at_ + n], sm[:, 2, at_:at_ + n], ACT.Sqrt).then_inc(sd_ready, 1)

            def squares(i, semaphore, value, src, at_):
                act.wait_ge(semaphore, value)
                if i:
                    act.wait_ge(sq_ready, i)
                for k in range(KB):
                    last = nc.scalar.activation(junk[:, k, :],
                                                src[:, k, :] if len(src.shape) == 3 else src[:, k // 4, k % 4, :], ACT.Square,
                                                accum_out=sm[:, 1, at_ + k:at_ + k + 1])
                last.then_inc(sq_ready, 1)

            def turned_out(n, i, src):
                act.wait_ge(xt_done[n], i + 1)
                if i >= 2:
                    act.wait_ge(xw_done[n], i - 1)
                nc.scalar.activation(xT[i % 2][:, :, :].rearrange("p q i -> p (q i)"), src,
                                     copy).then_inc(xT_ready[n], 1)

            def panel(s, p, par_, first, reused):
                for q in range(NS):
                    idx = q + (q >= BACK)
                    if q == 0 and reused and s == 0:
                        act.wait_ge(mask_made, (p - 1) * NB)
                    act.wait_ge(tr_done[s], p * NS + q + 1)
                    nc.scalar.activation(at[par_ if s == 0 else 1 - par_][:, :, q * PW:(q + 1) * PW],
                                         turn[(par_ + idx) % 2][:, :].rearrange("p (j c) -> p j c", j=JP),
                                         copy).then_inc(at_ready[s], 1)
                    if q == SQRT_SLOT and s == 1 and not first:
                        root(NVARS0 + p - 1, 0, JP)

            def bank_out(s, i):
                c = order(s)[i]
                act.wait_ge(bank_done[s], i + 1)
                nc.scalar.activation(hT[:, c * BANK:(c + 1) * BANK], hacc[:, c * BANK:(c + 1) * BANK],
                                     copy).then_inc(hT_ready[s], 1)

            for b in range(NB):
                turned_out(0, b, bank_of(b))
            panel(0, 0, 0, True, False)
            panel(0, 1, 1, False, False)
            with act.Fori(1, NP // 2) as h:
                panel(0, 2 * h, 0, False, True)
                panel(0, 2 * h + 1, 1, False, True)
            root(0, 0, K)
            for m in range(NB):
                act.wait_ge(mask_out[m], 16 * NP)
            bank_out(0, 0)
            bank_out(0, 1)
            for t in range(NB + 2):
                if t + 2 < NB:
                    bank_out(0, t + 2)
                if t < NB:
                    squares(max(2 * t - 1, 0), h_back[0], t + 1,
                            turn[t % 2][:, :].rearrange("p (q h f) -> p h q f", q=4, h=2), t * KB)
                if t >= 2:
                    turned_out(1, t - 2, bank_of(t - 2))
                if 1 <= t <= NB:
                    squares(min(2 * t, 2 * NB - 1), cen_ready, t, hg[(t - 1) % 2], (t - 1) * KB)
                if t <= NB:
                    root(1 + t, max(t - 1, 0) * KB, (1 if t in (0, NB) else 2) * KB)

            act.wait_ge(mask_made, NP * NB)
            act.sem_inc(at_ready[1], 2 * NS)
            root(NVARS0, 0, JP)
            with act.Fori(1, NP // 2) as h:
                panel(1, 2 * h, 0, False, True)
                panel(1, 2 * h + 1, 1, False, True)
            root(NVARS0 + NP - 1, 0, JP)
            for i in range(NB):
                bank_out(1, i)

            def groups_step(n):
                for i in due(n, T_ROOT):
                    root(NVARS0 + NP + i, order(1)[i] * KB, KB)
                for i in due(n, T_XT_OUT):
                    turned_out(2, i, pw3[i % 2][:, :])
                for i in due(n, T_HIGH):
                    act.wait_ge(xw_done[2], i + 1)
                    b = order(1)[i]
                    nc.scalar.activation(s2[:, b * KB:(b + 1) * KB, 0:F], pw3[i % 2][:, :].rearrange("p (n f) -> p n f", n=KB),
                                         copy, scale=W_UNIT).then_inc(high_ready, 1)

            def row_group(r, first):
                for n in range(K):
                    for c in range(2):
                        act.wait_ge(cnt_done, (r * K + n) * 2 + c + 1)
                        nc.scalar.activation(wbits[c][n % 2], cnt[c], ACT.Relu).then_inc(bits_ready, 1)
                    if n == 0 and not first:
                        sums_out(r - 1)
                    if first:
                        groups_step(n)
                    for c in range(2):
                        if n == FINISH + 16 * c + 2 * FROOT + 1 and not first:
                            root(NVARS0 + NVARS1 + 2 * (r - 1) + c, c * KB // 2, KB // 2)

            def sums_out(r):
                act.wait_ge(w_used, r * K + K)
                nc.scalar.activation(hT[:, 0:BANK], acc[0], copy).then_inc(oT_ready[0], 1)

            for n in range(-LEAD, 0):
                groups_step(n)
            row_group(0, True)
            with act.Fori(1, NB) as r:
                row_group(r, False)
            sums_out(NB - 1)
            root(NVARS0 + NVARS1 + 2 * (NB - 1), 0, KB)

        @block.vector
        def _(dve):
            V = nc.vector
            done = [0]

            def link(ins):
                done[0] = done[0] + 1
                ins.then_inc(chain, 1)
                dve.wait_ge(chain, done[0])

            def over_f(col, n):
                return col.rearrange("p (n a) -> p n a", a=1).broadcast_to([P, n, F])

            def over_n(row, n):
                return row.rearrange("p (a f) -> p a f", a=1).broadcast_to([P, n, F])

            def inverse_root(i, at_, n):
                v, sd, r0, u = (sm[:, c, at_:at_ + n] for c in (2, 3, 4, 5))
                dve.wait_ge(sd_ready, i + 1)
                link(V.reciprocal(r0, sd))
                link(V.scalar_tensor_tensor(u, r0, -0.5, r0, ALU.mult, ALU.mult))
                link(V.tensor_tensor(u, u, v, ALU.mult))
                link(V.scalar_tensor_tensor(u, u, 1.5, r0, ALU.add, ALU.mult))
                return u

            def less_mean(src, at_, n):
                mean = sm[:, 0, at_:at_ + n]
                link(V.tensor_reduce(mean, src, AX_X, ALU.add))
                link(V.tensor_scalar(mean, mean, 1.0 / F, None, ALU.mult))
                return V.tensor_tensor(src, src, over_f(mean, n), ALU.subtract)

            def variance(at_, n):
                V.tensor_scalar(sm[:, 2, at_:at_ + n], sm[:, 1, at_:at_ + n], 1.0 / F, LN_EPS,
                                ALU.mult, ALU.add).then_inc(var_ready, 1)

            dve.wait_ge(in_factors, 16 * 4)
            link(V.tensor_tensor(sm[:, 6, 0:1], par[:, 0:1], par[:, 1:2], ALU.mult))
            link(V.tensor_tensor(sm[:, 6, 1:2], par[:, 2:3], par[:, 3:4], ALU.mult))
            dve.wait_ge(dg_done, 1)
            link(V.tensor_scalar(g[:, 0:KU], tacc[:, 0:KU], sm[:, 6, 0:1], None, ALU.mult))
            link(V.tensor_scalar(g[:, KU:K], tacc[:, KU:K], sm[:, 6, 1:2], None, ALU.mult))

            def group(t, b):
                return t[:, b * KB:(b + 1) * KB, :]

            def bank(b):
                return hacc[:, b * BANK:(b + 1) * BANK].rearrange("p (n f) -> p n f", n=KB)

            for b in range(NB):
                dve.wait_ge(xw_done[0], b + 1)
                if b >= 2:
                    dve.wait_ge(v_ready[0], b - 1)
                link(V.tensor_tensor(hg[b % 2][:, :, :], bank(b), over_f(g[:, b * KB:(b + 1) * KB], KB), ALU.mult))
                dve.wait_ge(in_x[b], 16)
                V.tensor_tensor(group(ez, b), hg[b % 2][:, :, :], group(xa, b), ALU.add).then_inc(v_ready[0], 1)

            def take(s, p):
                dve.wait_ge(nat_used[s], (p + 1) * NG)
                return V.tensor_copy(tT[:, :], tacc[:, 0:PW]).then_inc(tT_ready[s], 1)

            def halves(par_):
                return turn[(par_ + BACK) % 2][:, 0:PW].rearrange("p (j h f) -> p j f h", j=JP, h=2)

            def masks(p, par_, m, first):
                rows_ = slice(m * RW, (m + 1) * RW)
                dve.wait_ge(at_ready[0], p * NS + MS * (m + 1))
                if not first:
                    dve.wait_ge(mask_out[m], p * 16)
                V.tensor_reduce(degp[:, bass.ds(p * JP, JP), m], at[par_][:, :, rows_], AX_X, ALU.add)
                V.tensor_scalar(mstage[m].rearrange("p (j r) -> p j r", j=JP), at[par_][:, :, rows_], 0.0, None,
                                ALU.not_equal, saturate=False).then_inc(mask_made, 1)

            def panel0(p, par_, first):
                if not first:
                    dve.wait_ge(back_done[0], p)
                    V.tensor_reduce(tv[1 - par_][:, :, :], halves(par_), AX_X, ALU.add).then_inc(tv_ready[0], 1)
                for m in range(NB - 1):
                    masks(p, par_, m, first)
                take(0, p)
                masks(p, par_, NB - 1, first)

            panel0(0, 0, True)
            panel0(1, 1, False)
            dve.wait_ge(in_late, 16 * 8)
            dve.wait_ge(consts, 12)
            V.tensor_tensor(centerg[:, :].rearrange("p (n f) -> p n f", n=2), center[:, :].rearrange("p (n f) -> p n f", n=2),
                            over_n(rows[:, 0, :], 2), ALU.mult).then_inc(centerg_ready, 1)
            with dve.Fori(1, NP // 2) as h:
                panel0(2 * h, 0, False)
                panel0(2 * h + 1, 1, False)
            dve.wait_ge(back_done[0], NP)
            V.tensor_reduce(tv[1][:, :, :], halves(0), AX_X, ALU.add).then_inc(tv_ready[0], 1)

            dve.wait_ge(mask_made, NP * NB)
            link(V.tensor_reduce(sm[:, 0, :], degp[:, :, :], AX_X, ALU.add))
            link(V.tensor_scalar(sm[:, 0, :], sm[:, 0, :], 1.0, None, ALU.add))
            link(V.tensor_scalar(dinv[:, :], sm[:, 0, :], 0.0, None, ALU.is_gt))
            V.tensor_scalar(sm[:, 2, :], sm[:, 0, :], 2.0 ** -100, None, ALU.max).then_inc(var_ready, 1)
            u = inverse_root(0, 0, K)
            link(V.tensor_tensor(dinv[:, :], u, dinv[:, :], ALU.mult))

            def turned_group(s, i):
                dve.wait_ge(h_back[s], i + 1)
                return turn[i % 2][:, :].rearrange("p (q h f) -> p h q f", q=4, h=2)

            def by_half(t):
                return t.rearrange("p (h q) f -> p h q f", h=2)

            def first_norm_ends(b):
                w = hg[b % 2][:, :, :]
                u = sm[:, 5, b * KB:(b + 1) * KB]
                dve.wait_ge(hg_back, b + 1)
                if b >= 2:
                    dve.wait_ge(x_ready[1], b - 1)
                for h in range(2):
                    src = bank(b).rearrange("p (q h) f -> p h q f", h=2)[:, h, :, :]
                    ins = V.tensor_tensor(w[:, 4 * h:4 * h + 4, :], src, over_f(u[:, 4 * h:4 * h + 4], 4), ALU.mult)
                link(ins)
                link(V.tensor_tensor(w, w, group(xb, b), ALU.add))
                less_mean(w, b * KB, KB).then_inc(cen_ready, 1)

            def make_z(b):
                dve.wait_ge(xw_done[1], b + 1)
                V.tensor_tensor(group(ez, b), bank(b), over_f(dinv[:, b * KB:(b + 1) * KB], KB),
                                ALU.mult).then_inc(v_ready[1], 1)

            dve.wait_ge(u_ready, 2)
            for t in range(NB + 2):
                lo, n = max(t - 1, 0) * KB, (1 if t in (0, NB) else 2) * KB
                if 1 <= t <= NB:
                    first_norm_ends(t - 1)
                if t >= 2:
                    make_z(t - 2)
                if t <= NB:
                    dve.wait_ge(sq_ready, min(2 * t + 1, 2 * NB))
                    variance(lo, n)
                    inverse_root(1 + t, lo, n)
                if 1 <= t <= NB:
                    b = t - 1
                    V.tensor_tensor(group(xb, b), hg[b % 2][:, :, :], over_f(sm[:, 5, b * KB:(b + 1) * KB], KB),
                                    ALU.mult).then_inc(x_ready[1], 1)

            def x2_of(p, par_, column_block):
                y, sq = x2_work, x2_work2
                dve.wait_ge(back_done[1], p)
                blk = bass.ds(column_block, JP)
                V.tensor_reduce(y, halves(par_), AX_X, ALU.add).then_inc(back_read[1], 1)
                dve.wait_ge(back_read[1], p)
                link(V.tensor_tensor(y, y, ez[:, blk, :], ALU.add))
                link(V.tensor_tensor(y, y, over_f(dinv[:, blk], JP), ALU.mult))
                link(V.tensor_tensor(y, y, over_n(rows[:, 2, :], JP), ALU.add))
                link(V.scalar_tensor_tensor(y, y, 0.0, xb[:, blk, :], ALU.max, ALU.add))
                link(less_mean(y, 0, JP))
                link(V.tensor_tensor(sq, y, y, ALU.mult))
                link(V.tensor_reduce(sm[:, 1, 0:JP], sq, AX_X, ALU.add))
                variance(0, JP)
                u = inverse_root(NVARS0 + p - 1, 0, JP)
                dst = tv[par_][:, :, :]
                V.tensor_tensor(dst, y, over_f(u, JP), ALU.mult).then_inc(tv_ready[1], 1)
                dve.wait_ge(tv_ready[1], p)
                V.tensor_copy(xa[:, blk, :], dst)
                link(V.tensor_scalar(sq, dst, -B_CONST, F_CONST, ALU.mult, ALU.add))
                link(V.tensor_tensor(xb[:, blk, :], sq, dst, ALU.add))

            X2_LINKS = 4 + 3 + 2 + 4 + 2

            take(1, 0)
            x2_of(1, 1, (NP - 1) * JP)
            take(1, 1)
            x2_of(2, 0, (NP - 2) * JP)
            take(1, 2)
            before = done[0]
            with dve.Fori(1, NP // 2 - 1) as h:
                done[0] = before + (2 * h - 2) * X2_LINKS
                x2_of(2 * h + 1, 1, (2 * h - 2) * JP)
                take(1, 2 * h + 1)
                x2_of(2 * h + 2, 0, (2 * h - 1) * JP)
                take(1, 2 * h + 2)
            done[0] = before + (NP - 4) * X2_LINKS
            x2_of(NP - 1, 1, (NP - 4) * JP)
            take(1, NP - 1)
            x2_of(NP, 0, (NP - 3) * JP)

            def groups_step(n):
                for i in due(n, T_PRODUCT):
                    b, w = order(1)[i], hg[i % 2][:, :, :]
                    src = turned_group(1, i)
                    if i >= 2:
                        dve.wait_ge(x_ready[2], i - 1)
                    V.tensor_tensor(by_half(w), src, by_half(group(xa, b)), ALU.mult).then_inc(h_read, 1)
                for i in due(n, T_OUTER):
                    b, w = order(1)[i], hg[i % 2][:, :, :]
                    outer = sm[:, 6, b * KB:(b + 1) * KB]
                    dve.wait_ge(h_read, i + 1)
                    link(V.tensor_reduce(outer, w, AX_X, ALU.add))
                    V.tensor_scalar(outer, outer, R_CONST, None, ALU.mult).then_inc(outer_ready, 1)
                for i in due(n, T_MEAN):
                    b, w = order(1)[i], hg[i % 2][:, :, :]
                    dve.wait_ge(less_outer, i + 1)
                    mean = sm[:, 0, b * KB:(b + 1) * KB]
                    link(V.tensor_reduce(mean, w, AX_X, ALU.add))
                    link(V.tensor_scalar(mean, mean, 1.0 / F, None, ALU.mult))
                for i in due(n, T_CENTER):
                    b, w = order(1)[i], hg[i % 2][:, :, :]
                    V.tensor_tensor(w, w, over_f(sm[:, 0, b * KB:(b + 1) * KB], KB), ALU.subtract).then_inc(cen_ready, 1)
                for i in due(n, T_VAR):
                    b = order(1)[i]
                    dve.wait_ge(sq3_ready, i + 1)
                    link(V.tensor_reduce(sm[:, 1, b * KB:(b + 1) * KB], junk[:, :, :], AX_X, ALU.add))
                    variance(b * KB, KB)
                for i in due(n, T_INVERSE):
                    inverse_root(NVARS0 + NP + i, order(1)[i] * KB, KB)
                for i in due(n, T_END):
                    b = order(1)[i]
                    V.tensor_tensor(group(xb, b), hg[i % 2][:, :, :], over_f(sm[:, 5, b * KB:(b + 1) * KB], KB),
                                    ALU.mult).then_inc(x_ready[2], 1)
                for i in due(n, T_LOW):
                    b = order(1)[i]
                    dve.wait_ge(high_ready, i + 1)
                    V.scalar_tensor_tensor(group(s2, b)[:, :, F:2 * F], pw3[i % 2][:, :].rearrange("p (n f) -> p n f", n=KB),
                                           W_UNIT, group(s2, b)[:, :, 0:F].bitcast(F32), ALU.mult,
                                           ALU.subtract).then_inc(v_ready[2], 1)

            for n in range(-LEAD, 0):
                groups_step(n)

            HK = KB // 2

            def finish(r, c, i, chunks=1):
                n = chunks * HK
                blk = bass.ds(r * KB + c * HK, n)
                o, sq = hg[0][:, c * HK:c * HK + n, :], hg[1][:, c * HK:c * HK + n, :]
                mean, ss = sm[:, 0, c * HK:c * HK + n], sm[:, 1, c * HK:c * HK + n]
                if i == 0:
                    for chunk in range(c, c + chunks):
                        dve.wait_ge(o_back, r * 2 + chunk + 1)
                        ins = V.tensor_reduce(hg[0][:, chunk * HK:(chunk + 1) * HK, :],
                                              turn[chunk][:, :].rearrange("p (q h f) -> p q f h", q=4, h=2), AX_X, ALU.add)
                    link(ins)
                elif i == 1:
                    link(V.tensor_tensor(o, o, xb[:, blk, :], ALU.add))
                elif i == 2:
                    link(V.tensor_reduce(mean, o, AX_X, ALU.add))
                    link(V.tensor_scalar(mean, mean, 1.0 / F, None, ALU.mult))
                elif i == 3:
                    link(V.tensor_tensor(o, o, over_f(mean, n), ALU.subtract))
                elif i == 4:
                    link(V.tensor_tensor(sq, o, o, ALU.mult))
                elif i == FROOT:
                    link(V.tensor_reduce(ss, sq, AX_X, ALU.add))
                    variance(c * HK, n)
                elif i == 6:
                    inverse_root(NVARS0 + NVARS1 + r * 2 + c, c * HK, n)
                elif i == 7:
                    V.tensor_tensor(xa[:, blk, :], o, over_f(sm[:, 5, c * HK:c * HK + n], n),
                                    ALU.mult).then_inc(y_ready, chunks)
                    dve.wait_ge(y_ready, r * 2 + c + chunks)

            FINISH_LINKS = 2 * (1 + 1 + 2 + 1 + 1 + 1 + 4)

            def row_group(r, first):
                for n in range(K):
                    for c in range(2):
                        dve.wait_ge(bits_ready, (r * K + n) * 2 + c + 1)
                        V.tensor_copy(wr[c][n % 2][:, :], wbits[c][n % 2].bitcast(BF16)).then_inc(w_ready, 1)
                    if first:
                        groups_step(n)
                    if n == 0 and not first:
                        sums_out(r - 1)
                    for c in range(2):
                        i, odd = divmod(n - FINISH - 16 * c, 2)
                        if not first and not odd and 0 <= i < FSTEPS:
                            finish(r - 1, c, i)

            def sums_out(r):
                dve.wait_ge(w_used, r * K + K)
                V.tensor_copy(hT[:, BANK:2 * BANK], acc[1]).then_inc(oT_ready[1], 1)

            row_group(0, True)
            dve.wait_ge(xb3_ready, 1)
            before = done[0]
            with dve.Fori(1, NB) as r:
                done[0] = before + (r - 1) * FINISH_LINKS
                row_group(r, False)
            done[0] = before + (NB - 1) * FINISH_LINKS
            sums_out(NB - 1)
            for i in range(FSTEPS):
                finish(NB - 1, 0, i, 2)


_INS = ['x', 'adj', 'L0_gnn_W_u', 'L0_gnn_diag_u', 'L0_gnn_par_u', 'L0_gnn_W_i', 'L0_gnn_diag_i', 'L0_gnn_par_i',
        'L0_gnn_ln_gamma', 'L0_gnn_ln_beta', 'L1_gnn_W', 'L1_gnn_b', 'L3_gnn_weight', 'L3_gnn_bias']


def kernel(**inputs):
    import numpy as _np
    import concourse.bacc as _bacc
    from concourse import mybir as _mybir
    from concourse.bass_utils import run_bass_kernel_spmd as _run

    nc = _bacc.Bacc("TRN2", target_bir_lowering=False, num_devices=1)
    arrays, args = {}, []
    for name in _INS:
        a = _np.ascontiguousarray(inputs[name])
        arrays[f"in_{name}"] = a
        args.append(nc.dram_tensor(f"in_{name}", a.shape, _mybir.dt.from_np(a.dtype), kind="ExternalInput").ap())
    shape = inputs['x'].shape
    args.append(nc.dram_tensor("out_x", shape, F32, kind="ExternalOutput").ap())
    resnorm_kernel(nc, *args)
    r = _run(nc, [arrays], core_ids=[0])
    return r.results[0]["out_x"]
```
